# Optimizing a Trainium2 kernel written in Bass

```python
import numpy as np
import jax
import jax.numpy as jnp

def _softmax(x, axis=-1):
    return jax.nn.softmax(x, axis=axis)

def _gelu(x):
    return jax.nn.gelu(x, approximate=True)

def _silu(x):
    return jax.nn.silu(x)

def _sigmoid(x):
    return jax.nn.sigmoid(x)

def _layernorm(x, axis=-1, eps=1e-05):
    m = jnp.mean(x, axis=axis, keepdims=True)
    v = jnp.var(x, axis=axis, keepdims=True)
    return (x - m) / jnp.sqrt(v + eps)

def _scatter_add(tgt, idx, src, axis=0):
    return tgt.at[idx].add(src)

def _segment_sum(src, seg, n):
    return jax.ops.segment_sum(src, seg, n)
kernel_name = 'mk_lm_tower_d1_tok_ids1024_r4_fee1c9'

def setup_inputs(seed: int=0):
    np.random.seed(seed)
    _w = jnp.asarray

    def _rec_inputs():
        import jax
        import jax.numpy as jnp
        _rk = jax.random.key(seed)
        x = jax.random.randint(jax.random.fold_in(_rk, 1), (8, 256), 0, 31993, jnp.int32)
        return x
    x = _rec_inputs()

    def _L0_tok_setup():
        import jax, jax.numpy as jnp
        import numpy as np
        VOCAB_SIZE = 8000
        EMBED_DIM = 256

        def _trunc_normal(key, shape, lo=-3.0, hi=3.0):
            return jax.random.truncated_normal(key, lo, hi, shape, dtype=jnp.float32)
        key = jax.random.key(seed)
        k_x, k_w = jax.random.split(key)
        x = jax.random.randint(k_x, (4, 512), 0, VOCAB_SIZE, dtype=jnp.int64 if jax.config.read('jax_enable_x64') else jnp.int32)
        embeddings = _trunc_normal(k_w, (VOCAB_SIZE, EMBED_DIM))
        return {'x': x, 'embeddings': embeddings}
    _L0_tok_all = _L0_tok_setup()
    _L0_tok_in = {k: v for k, v in _L0_tok_all.items() if k in ('embeddings',)}
    del _L0_tok_all

    def _L0_attn_setup():
        import jax, jax.numpy as jnp
        import numpy as np
        N_HEADS = 16

        def _rotate_half(t):
            shp = t.shape
            t2 = t.reshape(*shp[:-1], shp[-1] // 2, 2)
            return jnp.stack((-t2[..., 1], t2[..., 0]), axis=-1).reshape(shp)
        key = jax.random.key(seed)
        k1, k2, k3 = jax.random.split(key, 3)
        B, N, D = (2, 512, 256)
        x = jax.random.normal(k1, (B, N, D), dtype=jnp.float32)
        w_qkv = jax.random.normal(k2, (D, 3 * D), dtype=jnp.float32) * D ** (-0.5)
        w_proj = jax.random.normal(k3, (D, D), dtype=jnp.float32) * D ** (-0.5)
        return {'x': x, 'w_qkv': w_qkv, 'w_proj': w_proj}
    _L0_attn_all = _L0_attn_setup()
    _L0_attn_in = {k: v for k, v in _L0_attn_all.items() if k in ('w_qkv', 'w_proj')}
    del _L0_attn_all

    def _L0_ffn_setup():
        import jax, jax.numpy as jnp
        import numpy as np
        B, S, H, E = (2, 2048, 256, 8)
        SCALE = 0.5
        key = jax.random.key(seed)
        k1, k2 = jax.random.split(key)
        x = jax.random.normal(k1, (B, S, H), dtype=jnp.float32)
        gate_w = jax.random.normal(k2, (E, H), dtype=jnp.float32) * 0.02
        coeff = SCALE * (1.0 + 0.05 * jnp.arange(E, dtype=jnp.float32))
        expert_w = coeff[:, None, None] * jnp.eye(H, dtype=jnp.float32)
        return {'x': x, 'gate_w': gate_w, 'expert_w': expert_w}
    _L0_ffn_all = _L0_ffn_setup()
    _L0_ffn_in = {k: v for k, v in _L0_ffn_all.items() if k in ('gate_w', 'expert_w')}
    del _L0_ffn_all
    return {'x': x, 'L0_tok_embeddings': _L0_tok_in['embeddings'], 'L0_attn_w_qkv': _L0_attn_in['w_qkv'], 'L0_attn_w_proj': _L0_attn_in['w_proj'], 'L0_ffn_gate_w': _L0_ffn_in['gate_w'], 'L0_ffn_expert_w': _L0_ffn_in['expert_w']}

def reference(x, L0_tok_embeddings, L0_attn_w_qkv, L0_attn_w_proj, L0_ffn_gate_w, L0_ffn_expert_w):
    import jax
    import jax.numpy as jnp

    def _L0_tok_ref(x, embeddings):
        import jax, jax.numpy as jnp
        import numpy as np
        VOCAB_SIZE = 8000
        EMBED_DIM = 256

        def _trunc_normal(key, shape, lo=-3.0, hi=3.0):
            return jax.random.truncated_normal(key, lo, hi, shape, dtype=jnp.float32)
        vocab_size = embeddings.shape[0]
        onehot = (x[..., None] == jnp.arange(vocab_size)).astype(embeddings.dtype)
        return jnp.einsum('...v,vd->...d', onehot, embeddings)

    def _L0_attn_ref(x, w_qkv, w_proj):
        import jax, jax.numpy as jnp
        import numpy as np
        N_HEADS = 16

        def _rotate_half(t):
            shp = t.shape
            t2 = t.reshape(*shp[:-1], shp[-1] // 2, 2)
            return jnp.stack((-t2[..., 1], t2[..., 0]), axis=-1).reshape(shp)
        B, N, D = x.shape
        H = N_HEADS
        hd = D // H
        qkv = x @ w_qkv
        qkv = qkv.reshape(B, N, 3, H, hd).transpose(2, 0, 3, 1, 4)
        q, k, v = (qkv[0], qkv[1], qkv[2])
        inv_freq = 1.0 / 10000.0 ** (jnp.arange(0, hd, 2, dtype=jnp.float32) / hd)
        freqs = jnp.arange(N, dtype=jnp.float32)[:, None] * inv_freq[None, :]
        sin = jnp.repeat(jnp.sin(freqs), 2, axis=-1)[None, None]
        cos = jnp.repeat(jnp.cos(freqs), 2, axis=-1)[None, None]
        q = q * cos + _rotate_half(q) * sin
        k = k * cos + _rotate_half(k) * sin
        scale = hd ** (-0.5)
        attn = jax.nn.softmax(jnp.einsum('bhqd,bhkd->bhqk', q, k) * scale, axis=-1)
        out = jnp.einsum('bhqk,bhkd->bhqd', attn, v)
        out = out.transpose(0, 2, 1, 3).reshape(B, N, D)
        return out @ w_proj

    def _L0_ffn_ref(x, gate_w, expert_w):
        import jax, jax.numpy as jnp
        import numpy as np
        B, S, H, E = (2, 2048, 256, 8)
        SCALE = 0.5
        scores = jnp.einsum('bsh,eh->bse', x, gate_w)
        chosen = jnp.argmax(scores, axis=-1)
        onehot = jax.nn.one_hot(chosen, gate_w.shape[0], dtype=x.dtype)
        expert_out = jnp.einsum('bsh,efh->bsef', x, expert_w)
        return x + jnp.einsum('bsef,bse->bsf', expert_out, onehot)
    h = _L0_tok_ref(x, L0_tok_embeddings)
    h = h + _L0_attn_ref(_layernorm(h, axis=-1), L0_attn_w_qkv, L0_attn_w_proj)
    h = h + _L0_ffn_ref(_layernorm(h, axis=-1), L0_ffn_gate_w, L0_ffn_expert_w)
    return h

_drawn_inputs = setup_inputs


def setup_inputs(seed=0):
    import zlib

    import numpy as np

    out = dict(_drawn_inputs(seed))
    spreads = {}
    factors = {}
    for name, (base, spread) in spreads.items():
        noise = np.random.default_rng([zlib.crc32(name.encode()), seed]).standard_normal(out[name].shape)
        drawn = base * np.exp(spread * noise) if base else spread * noise
        out[name] = jnp.asarray(drawn.astype(out[name].dtype))
    for name, factor in factors.items():
        out[name] = (out[name] * factor).astype(out[name].dtype)
    return out
```

```python
from contextlib import ExitStack

import numpy as np

import concourse.bass as bass
from concourse import mybir

F32 = mybir.dt.float32
F32R = mybir.dt.float32r
I32 = mybir.dt.int32
U32 = mybir.dt.uint32
ALU = mybir.AluOpType
ACT = mybir.ActivationFunctionType
AX = mybir.AxisListType

P = 128
EPS = 1e-5
RING = 8
STRIP = 32
PARTS = 4
N_EXP = 8


def rope_tables(n, hd):
    inv = (1.0 / np.float32(10000.0) ** (np.arange(0, hd, 2, dtype=np.float32) / np.float32(hd))).astype(np.float32)
    angle = np.arange(n, dtype=np.float32)[:, None] * inv[None, :]
    cos = np.repeat(np.cos(angle), 2, axis=-1)
    sin = np.repeat(np.sin(angle), 2, axis=-1)
    sin[:, 0::2] *= -1
    both = np.stack([cos, sin], axis=1).astype(np.float32)
    return np.ascontiguousarray(both.reshape(n // P, P, 2, hd).transpose(1, 0, 2, 3))


def tower(nc, x, emb, w_qkv, w_proj, gate_w, expert_w, rope, ramp, out):
    NB, N, _ = out.shape
    V, D = emb.shape
    HD = rope.shape[3]
    NH = D // HD
    NT = N // P
    C = D // P
    PAIRS = NH // 2
    GROUPS = NH // 4
    HALF = PAIRS // 2
    SCALE = float(HD) ** -0.5
    KS = 3 * HD
    KM = KS + 2
    assert NT == 2 and C == 2 and NH == 16 and HD == 16 and NB % 2 == 0

    with ExitStack() as ctx:
        def sb(name, shape, dt=F32):
            return ctx.enter_context(nc.sbuf_tensor(name, shape, dt))

        def bank(name):
            return ctx.enter_context(nc.psum_tensor(name, [P, 512], F32))

        def sem(name):
            return ctx.enter_context(nc.semaphore(name))

        rope_sb = sb("rope_sb", [P, NT, 2, HD])
        ramp_sb = sb("ramp_sb", [P, N_EXP])
        ident = sb("ident", [P, P])
        ident_r = sb("ident_r", [P, P], F32R)
        neg_half = sb("neg_half", [P, NT])
        wqkv_h = sb("wqkv_h", [P, C, 3 * D], F32R)
        wqkv_l = sb("wqkv_l", [P, C, 3 * D], F32R)
        wp_h = sb("wp_h", [P, C, D], F32R)
        wp_l = sb("wp_l", [P, C, D], F32R)
        ew_raw = sb("ew_raw", [P, C, N_EXP * D])
        ew_h = sb("ew_h", [P, C, N_EXP * D], F32R)
        ew_l = sb("ew_l", [P, C, N_EXP * D], F32R)
        gw_raw = sb("gw_raw", [P, C, N_EXP])
        gw_h = sb("gw_h", [P, C, N_EXP], F32R)
        gw_l = sb("gw_l", [P, C, N_EXP], F32R)
        ids = sb("ids", [P, NB * NT], I32)
        h0 = sb("h0", [P, NB * NT, D])
        f_st = sb("f_st", [P, NT, 6])
        f_mv = sb("f_mv", [P, NT, 2])
        f_ve = sb("f_ve", [P, NT])
        f_rs = sb("f_rs", [P, NT])
        xn = sb("xn", [P, NT, D])
        x_h = sb("x_h", [P, C, NT, P], F32R)
        x_l = sb("x_l", [P, C, NT, P], F32R)
        rope_a = sb("rope_a", [P, NT, 2 * NH, HD])
        rope_b = sb("rope_b", [P, NT, 2 * NH, HD])
        qk = sb("qk", [P, NT, 2 * NH, HD])
        parts = sb("parts", [P, NT, 2 * NH, PARTS, HD], F32R)
        q_stack = [sb(f"q_stack{i}", [P, PAIRS, N], F32R) for i in range(2)]
        k_stack = [sb(f"k_stack{i}", [P, PAIRS, N], F32R) for i in range(2)]
        vals = [sb(f"vals{i}", [P, NT, NH, STRIP]) for i in range(2)]
        neg_max = sb("neg_max", [P, 2, NT, 2, HALF])
        max_parts = sb("max_parts", [P, 2, NT, 2, 2, HALF], F32R)
        max_rows = sb("max_rows", [4 * HALF, 2, N], F32R)
        probs = sb("probs", [P, RING, NT, N])
        wqkv_raw = probs[:, 0:3, :, :].rearrange("p r t n -> p (r t n)").rearrange("p (c n) -> p c n", c=C)
        wp_raw = probs[:, 3, :, :]
        o_t = sb("o_t", [P, GROUPS, N])
        o_rs = sb("o_rs", [P, NT, NH])
        o_n = sb("o_n", [P, NT, NH, HD])
        o_h = sb("o_h", [P, C, NT, P], F32R)
        o_l = sb("o_l", [P, C, NT, P], F32R)
        h1 = sb("h1", [P, NT, D])
        g_st = sb("g_st", [P, NT, 6])
        g_mv = sb("g_mv", [P, NT, 2])
        g_ve = sb("g_ve", [P, NT])
        g_rs = sb("g_rs", [P, NT])
        yn = sb("yn", [P, NT, D])
        y_h = sb("y_h", [P, C, NT, P], F32R)
        y_l = sb("y_l", [P, C, NT, P], F32R)
        base = sb("base", [P, NT, D])
        score = sb("score", [P, NT, N_EXP])
        top = sb("top", [P, NT, 8])
        top_at = sb("top_at", [P, NT, 8], U32)
        mask = sb("mask", [P, NT, N_EXP])
        acc = sb("acc", [P, 2, NT, D])
        res = sb("res", [P, NT, D])

        s_bank = [bank("s_bank0"), bank("s_bank1")]
        f_bank = bank("f_bank")
        t_bank = [bank("t_bank0"), bank("t_bank1")]
        o_bank = bank("o_bank")
        m_bank = [bank("m_bank0"), bank("m_bank1")]

        ids_in, rope_in, wqkv_in, wp_in, ew_in, gw_in = map(sem, "ids_in rope_in wqkv_in wp_in ew_in gw_in".split())
        gathered = [sem(f"gathered{b}") for b in range(NB)]
        h_in = sem("h_in")
        h_zero, filled, pool_filled, ident_ok, identr_ok = map(sem, "h_zero filled pool_filled ident_ok identr_ok".split())
        wqkv_h_ok, wqkv_l_ok, wp_h_ok, wp_l_ok = map(sem, "wqkv_h_ok wqkv_l_ok wp_h_ok wp_l_ok".split())
        ew_h_ok, ew_l_ok, gw_h_ok, gw_l_ok = map(sem, "ew_h_ok ew_l_ok gw_h_ok gw_l_ok".split())
        f_stats, f_moments, f_var, f_rstd, f_normed = map(sem, "f_stats f_moments f_var f_rstd f_normed".split())
        xt_ps, xh_ok, xl_ok, v_ps, v_ok, qk_ps = map(sem, "xt_ps xh_ok xl_ok v_ps v_ok qk_ps".split())
        roped, rotated, part_h, part_d, part_l = map(sem, "roped rotated part_h part_d part_l".split())
        stack_ps, stack_ok = map(sem, "stack_ps stack_ok".split())
        s_ps, max_ok, mh_ok, ml_ok, mt_ps, mt_ok = map(sem, "s_ps max_ok mh_ok ml_ok mt_ps mt_ok".split())
        m_in = [sem("m_in0"), sem("m_in1")]
        t_ps, exp_ok, o_ps, o_ok = map(sem, "t_ps exp_ok o_ps o_ok".split())
        ot_ps, ors_ok, on_ok, ont_ps, oh_ok, ol_ok, proj_ps, h1_ok = map(
            sem, "ot_ps ors_ok on_ok ont_ps oh_ok ol_ok proj_ps h1_ok".split())
        g_stats, g_moments, g_var, g_rstd, g_normed, base_ok = map(
            sem, "g_stats g_moments g_var g_rstd g_normed base_ok".split())
        yt_ps, yh_ok, yl_ok, gate_ps, score_ok, top_ok, at_ok, mask_ok = map(
            sem, "yt_ps yh_ok yl_ok gate_ps score_ok top_ok at_ok mask_ok".split())
        exp_ps, acc_ok, res_ok, out_ok = map(sem, "expert_ps acc_ok res_ok out_ok".split())

        def steps(engine, step, post):
            step(0, True, False)
            with engine.Fori(0, (NB - 2) // 2) as i:
                step(i * 2 + 1, True, True, 1)
                step(i * 2 + 2, True, True, 0)
            step(NB - 1, False, True)
            post(NB - 1)

        def wait(engine, semaphore, value):
            if not isinstance(value, int) or value > 0:
                engine.wait_ge(semaphore, value)

        def wait_apart(engine, semaphore, value):
            if not isinstance(value, int):
                value = engine.snap(engine.to_reg(value))
            engine.wait_ge(ident_ok, 1)
            wait(engine, semaphore, value)

        block = ctx.enter_context(nc.Block())

        @block.sync
        def _(sp):
            sp.dma_start(ids[:, :], x).then_inc(ids_in, 16)
            sp.dma_start(wqkv_raw, w_qkv.rearrange("(c p) n -> p c n", p=P)).then_inc(wqkv_in, 16)
            sp.dma_start(rope_sb[:, :, :, :], rope).then_inc(rope_in, 16)
            sp.dma_start(ramp_sb[:, :], ramp).then_inc(rope_in, 16)
            sp.dma_start(wp_raw, w_proj.rearrange("(c p) n -> p c n", p=P)).then_inc(wp_in, 16)
            sp.dma_start(gw_raw[:, :, :], gate_w).then_inc(gw_in, 16)
            sp.dma_start(ew_raw[:, :, :], expert_w).then_inc(ew_in, 16)

            def landed(b):
                sp.wait_ge(gathered[b], 16 * NT)
                sp.sem_inc(h_in, 1)

            def maximum(b, p):
                for u in range(2):
                    wait(sp, mt_ok, b * 2 + u + 1)
                    for par in range(2):
                        r = 64 * par + KS
                        sp.dma_start(q_stack[p][r:r + 2, HALF * u:HALF * u + HALF, :].bitcast(F32),
                                     max_rows[2 * HALF * par:2 * HALF * (par + 1), u, :].bitcast(F32)).then_inc(m_in[u], 16)

            def post(b):
                wait(sp, res_ok, b + 1)
                sp.dma_start(out[b].rearrange("(t p) d -> p t d", p=P), res[:, :, :]).then_inc(out_ok, 16)

            def step(b, front, last, p=None):
                p = b % 2 if p is None else p
                if front:
                    maximum(b + 1, 1 - p)
                if last:
                    post(b - 1)

            landed(0)
            landed(1)
            maximum(0, 0)
            for b in range(2, NB):
                landed(b)
            steps(sp, step, post)
            sp.wait_ge(out_ok, 16 * NB)

        @block.gpsimd
        def _(pool):
            g = nc.gpsimd
            g.memset(ident[:, :], 0.0).then_inc(pool_filled, 1)
            g.memset(neg_half[:, :], -0.5).then_inc(pool_filled, 1)
            pool.wait_ge(pool_filled, 2)
            g.affine_select(out=ident[:, :], in_=ident[:, :], compare_op=ALU.not_equal, fill=1.0, base=0,
                            pattern=[[-1, P]], channel_multiplier=1).then_inc(ident_ok, 1)
            pool.wait_ge(ids_in, 16)
            for j in range(NB * NT):
                pool.wait_ge(h_zero, j // NT + 1)
                g.indirect_dma_start(h0[:, j, :], None, emb, bass.IndirectOffsetOnAxis(ap=ids[:, j:j + 1], axis=0),
                                     bounds_check=V - 1, oob_is_err=False).then_inc(gathered[j // NT], 16)

            def front(b):
                wait_apart(pool, f_moments, b * NT + NT)
                g.tensor_scalar(f_ve[:, :], f_mv[:, :, 1], EPS, None, ALU.add).then_inc(f_var, 1)
                wait(pool, f_var, b + 1)
                g.tensor_tensor(f_rs[:, :], f_ve[:, :], neg_half[:, :], ALU.pow).then_inc(f_rstd, 1)
                for t in range(NT):
                    wait_apart(pool, rotated, b * NT + t + 1)
                    g.tensor_copy(parts[:, t, 0:NH, 2, :], qk[:, t, 0:NH, :]).then_inc(part_d, 1)
                    g.tensor_copy(parts[:, t, NH:2 * NH, 1, :], qk[:, t, NH:2 * NH, :]).then_inc(part_d, 1)

            def post(b):
                wait_apart(pool, g_moments, b * NT + NT)
                g.tensor_scalar(g_ve[:, :], g_mv[:, :, 1], EPS, None, ALU.add).then_inc(g_var, 1)
                wait(pool, g_var, b + 1)
                g.tensor_tensor(g_rs[:, :], g_ve[:, :], neg_half[:, :], ALU.pow).then_inc(g_rstd, 1)
                wait(pool, g_normed, b * NT + NT)
                g.tensor_tensor(base[:, :, :], h1[:, :, :], yn[:, :, :], ALU.add).then_inc(base_ok, 1)

            def finish(b):
                wait(pool, acc_ok, b * 16 + 16)
                wait(pool, out_ok, b * 16)
                g.tensor_tensor(res[:, :, :], acc[:, 0, :, :], acc[:, 1, :, :], ALU.add).then_inc(res_ok, 1)

            def expert_weights():
                pool.wait_ge(gw_h_ok, 1)
                g.tensor_tensor(gw_l[:, :, :], gw_raw[:, :, :], gw_h[:, :, :].bitcast(F32), ALU.subtract).then_inc(gw_l_ok, 1)
                for k in range(8):
                    pool.wait_ge(ew_h_ok, k + 1)
                    w = slice(k % 4 * 2 * D, (k % 4 + 1) * 2 * D)
                    g.tensor_tensor(ew_l[:, k // 4, w], ew_raw[:, k // 4, w], ew_h[:, k // 4, w].bitcast(F32),
                                    ALU.subtract).then_inc(ew_l_ok, 1)

            def step(b, f, last, p=None):
                if f:
                    front(b + 1)
                if not last:
                    expert_weights()
                if last:
                    post(b - 1)
                    finish(b - 1)

            def tail(b):
                post(b)
                finish(b)

            front(0)
            steps(pool, step, tail)

        @block.tensor
        def _(pe):
            mm = nc.tensor.matmul
            tr = nc.tensor.transpose

            def product(o, xh, xl, wh, wl):
                n = 0
                for c in range(C):
                    for a, w in ((xh, wh), (xl, wh), (xh, wl)):
                        m = mm(o, a(c), w(c), start=(n == 0), stop=(n == 3 * C - 1))
                        n += 1
                return m

            def x_transpose(b):
                wait(pe, mt_ok, b * 2)
                wait(pe, f_normed, b * NT + NT)
                for c in range(C):
                    for t in range(NT):
                        k = (c * NT + t) * P
                        m = tr(f_bank[:, k:k + P], xn[:, t, c * P:(c + 1) * P], ident[:, :])
                m.then_inc(xt_ps, 1)

            def project(b):
                wait(pe, xl_ok, b + 1)
                for t in range(NT):
                    m = product(f_bank[:, t * D:(t + 1) * D], lambda c: x_h[:, c, t, :], lambda c: x_l[:, c, t, :],
                                lambda c: wqkv_h[:, c, 2 * D:3 * D], lambda c: wqkv_l[:, c, 2 * D:3 * D])
                m.then_inc(v_ps, 1)
                wait(pe, max_ok, b * NH)
                for t in range(NT):
                    product(s_bank[t][:, :], lambda c: x_h[:, c, t, :], lambda c: x_l[:, c, t, :],
                            lambda c: wqkv_h[:, c, 0:2 * D], lambda c: wqkv_l[:, c, 0:2 * D]).then_inc(qk_ps, 1)

            def stack(b, k):
                t, kind, half = k // 4, k % 4 // 2, k % 2
                if k % 4 == 0:
                    wait(pe, part_h, b * NT + t + 1)
                    wait(pe, part_d, b * 2 * NT + 2 * t + 2)
                    wait(pe, part_l, b * 2 * NT + 2 * t + 2)
                if k < 2:
                    wait(pe, roped, b * 2 * NT + 2 * NT)
                else:
                    wait(pe, stack_ok, b * 8 + k - 1)
                for j in range(HALF):
                    h = kind * NH + 2 * (half * HALF + j)
                    m = tr(s_bank[k % 2][:, j * P:(j + 1) * P].bitcast(F32R),
                           parts[:, t, h:h + 2, :, :].rearrange("p h a d -> p (h a d)"), ident_r[:, :])
                m.then_inc(stack_ps, 1)

            def scores(b, p, h):
                if h == 0:
                    wait(pe, stack_ok, b * 8 + 8)
                if h >= 2:
                    wait(pe, max_ok, b * NH + h - 1)
                r = 64 * (h % 2)
                for t in range(NT):
                    m = mm(s_bank[h % 2][:, t * N:(t + 1) * N], q_stack[p][r:r + KS, h // 2, t * P:(t + 1) * P],
                           k_stack[p][r:r + KS, h // 2, :], start=True, stop=True)
                m.then_inc(s_ps, 1)

            def max_transpose(b, u):
                if u == 0:
                    wait(pe, v_ok, b + 1)
                wait(pe, mt_ok, b * 2 + u)
                wait(pe, ml_ok, b * 2 + u + 1)
                for t in range(NT):
                    m = tr(f_bank[0:4 * HALF, t * P:(t + 1) * P].bitcast(F32R),
                           max_parts[:, u, t, :, :, :].rearrange("p a b c -> p (a b c)"), ident_r[:, :])
                m.then_inc(mt_ps, 1)

            def t_scores(b, p, h):
                if h % 8 == 0:
                    wait(pe, m_in[h // 8], b * 32 + 32)
                wait(pe, exp_ok, b * NH + h - 1)
                r = 64 * (h % 2)
                for c in range(NT):
                    m = mm(t_bank[h % 2][:, c * N:(c + 1) * N], k_stack[p][r:r + KM, h // 2, c * P:(c + 1) * P],
                           q_stack[p][r:r + KM, h // 2, :], start=True, stop=True)
                m.then_inc(t_ps, 1)

            def outputs(b, p, g):
                wait(pe, exp_ok, b * NH + 4 * g + 4)
                wait(pe, o_ok, b * GROUPS + g)
                for c in range(NT):
                    for j in range(4):
                        m = mm(o_bank[STRIP * j:STRIP * (j + 1), 0:N], vals[p][:, c, 4 * g + j, :],
                               probs[:, (4 * g + j) % RING, c, :], start=(c == 0), stop=(c == NT - 1),
                               skip_group_check=True)
                m.then_inc(o_ps, 1)

            def o_transpose(b):
                wait(pe, o_ok, b * GROUPS + GROUPS)
                wait(pe, acc_ok, b * 16)
                for t in range(NT):
                    for g in range(GROUPS):
                        m = tr(m_bank[t][:, g * P:(g + 1) * P], o_t[:, g, t * P:(t + 1) * P], ident[:, :])
                    m.then_inc(ot_ps, 1)

            def on_transpose(b):
                wait(pe, on_ok, b * NT + NT)
                for c in range(C):
                    for t in range(NT):
                        k = (c * NT + t) * P
                        m = tr(m_bank[0][:, k:k + P],
                               o_n[:, t, c * NH // C:(c + 1) * NH // C, :].rearrange("p h d -> p (h d)"), ident[:, :])
                m.then_inc(ont_ps, 1)

            def out_project(b):
                wait(pe, ol_ok, b + 1)
                for t in range(NT):
                    m = product(m_bank[1][:, t * D:(t + 1) * D], lambda c: o_h[:, c, t, :], lambda c: o_l[:, c, t, :],
                                lambda c: wp_h[:, c, :], lambda c: wp_l[:, c, :])
                m.then_inc(proj_ps, 1)

            def y_transpose(b):
                wait(pe, g_normed, b * NT + NT)
                for c in range(C):
                    for t in range(NT):
                        k = (c * NT + t) * P
                        m = tr(m_bank[0][:, k:k + P], yn[:, t, c * P:(c + 1) * P], ident[:, :])
                m.then_inc(yt_ps, 1)

            def gate(b):
                wait(pe, yl_ok, b + 1)
                for t in range(NT):
                    m = product(m_bank[1][:, t * N_EXP:(t + 1) * N_EXP], lambda c: y_h[:, c, t, :],
                                lambda c: y_l[:, c, t, :], lambda c: gw_h[:, c, :], lambda c: gw_l[:, c, :])
                m.then_inc(gate_ps, 1)

            def experts(b, n):
                u, t = n // NT, n % NT
                if n == 0:
                    wait(pe, score_ok, b + 1)
                if n >= 2:
                    wait(pe, acc_ok, b * 16 + 2 * (n - 2) + 2)
                product(m_bank[t][:, :], lambda c: y_h[:, c, t, :], lambda c: y_l[:, c, t, :],
                        lambda c: ew_h[:, c, 2 * u * D:2 * (u + 1) * D],
                        lambda c: ew_l[:, c, 2 * u * D:2 * (u + 1) * D]).then_inc(exp_ps, 1)

            def step(b, front, last, p=None):
                p = b % 2 if p is None else p
                for s in range(8):
                    t_scores(b, p, 2 * s)
                    t_scores(b, p, 2 * s + 1)
                    if last:
                        if s == 0:
                            o_transpose(b - 1)
                        if s == 1:
                            on_transpose(b - 1)
                        if s == 2:
                            out_project(b - 1)
                        if s == 3:
                            y_transpose(b - 1)
                        if s == 4:
                            gate(b - 1)
                        if s >= 5:
                            for n in range(*((0, 2), (2, 5), (5, 8))[s - 5]):
                                experts(b - 1, n)
                    if front:
                        if s == 0:
                            x_transpose(b + 1)
                        if s == 1:
                            project(b + 1)
                        if s in (2, 3):
                            for k in range(4 * (s - 2), 4 * (s - 2) + 4):
                                stack(b + 1, k)
                        if s >= 4:
                            for h in range(4 * (s - 4), 4 * (s - 4) + 4):
                                scores(b + 1, 1 - p, h)
                        if s == 6:
                            max_transpose(b + 1, 0)
                    if s % 2 == 0 and s > 0:
                        outputs(b, p, s // 2 - 1)
                outputs(b, p, 3)
                if front:
                    max_transpose(b + 1, 1)
                if not last:
                    pe.wait_ge(gw_l_ok, 1)
                    pe.wait_ge(ew_l_ok, N_EXP)

            def post(b):
                o_transpose(b)
                on_transpose(b)
                out_project(b)
                y_transpose(b)
                gate(b)
                for n in range(8):
                    experts(b, n)

            pe.wait_ge(ident_ok, 1)
            pe.wait_ge(identr_ok, 1)
            pe.wait_ge(filled, NT + 3)
            x_transpose(0)
            pe.wait_ge(wqkv_l_ok, C)
            project(0)
            for k in range(8):
                stack(0, k)
            for h in range(NH):
                scores(0, 0, h)
                if h == 9:
                    max_transpose(0, 0)
            max_transpose(0, 1)
            pe.wait_ge(wp_l_ok, 1)
            steps(pe, step, post)

        @block.scalar
        def _(act):
            def copy(o, i):
                return nc.scalar.activation(o, i, ACT.Copy)

            def x_high(b):
                wait(act, xt_ps, b + 1)
                copy(x_h[:, :, :, :].rearrange("p c t n -> p (c t n)"), f_bank[:, :]).then_inc(xh_ok, 1)

            def values(b, p):
                wait(act, v_ps, b + 1)
                copy(vals[p][:, :, :, 0:HD], f_bank[:, :].rearrange("p (t h d) -> p t h d", t=NT, h=NH)).then_inc(v_ok, 1)

            def high(b, t):
                wait(act, rotated, b * NT + t + 1)
                copy(parts[:, t, :, 0, :], qk[:, t, :, :]).then_inc(part_h, 1)

            def stack(b, p, k):
                t, kind, half = k // 4, k % 4 // 2, k % 2
                wait(act, stack_ps, b * 8 + k + 1)
                to = (q_stack, k_stack)[kind][p]
                copy(to[:, half * HALF:(half + 1) * HALF, t * P:(t + 1) * P],
                     s_bank[k % 2][:, :].rearrange("p (j n) -> p j n", j=HALF)).then_inc(stack_ok, 1)

            def max_row(b, u):
                wait(act, mt_ps, b * 2 + u + 1)
                copy(max_rows[:, u, :], f_bank[0:4 * HALF, 0:N]).then_inc(mt_ok, 1)

            def exp(b, h):
                wait(act, t_ps, b * NH + h + 1)
                if h % 4 == 0:
                    wait(act, o_ps, b * GROUPS + h // 4 - 1)
                nc.scalar.activation(probs[:, h % RING, :, :].rearrange("p c n -> p (c n)"), t_bank[h % 2][:, :],
                                     ACT.Exp, scale=SCALE).then_inc(exp_ok, 1)

            def outputs(b, g):
                wait(act, o_ps, b * GROUPS + g + 1)
                if g == 0:
                    wait(act, ot_ps, b * NT)
                copy(o_t[:, g, :], o_bank[:, 0:N]).then_inc(o_ok, 1)

            def o_high(b):
                wait(act, ont_ps, b + 1)
                copy(o_h[:, :, :, :].rearrange("p c t n -> p (c t n)"), m_bank[0][:, :]).then_inc(oh_ok, 1)

            def y_high(b):
                wait(act, yt_ps, b + 1)
                copy(y_h[:, :, :, :].rearrange("p c t n -> p (c t n)"), m_bank[0][:, :]).then_inc(yh_ok, 1)

            def expert_weights(k):
                if k == 0:
                    act.wait_ge(ew_in, 16)
                w = slice(k % 4 * 2 * D, (k % 4 + 1) * 2 * D)
                copy(ew_h[:, k // 4, w], ew_raw[:, k // 4, w]).then_inc(ew_h_ok, 1)

            def step(b, front, last, p=None):
                p = b % 2 if p is None else p
                for s in range(8):
                    exp(b, 2 * s)
                    exp(b, 2 * s + 1)
                    if last:
                        if s == 1:
                            o_high(b - 1)
                        if s == 3:
                            y_high(b - 1)
                    else:
                        expert_weights(s)
                    if front:
                        if s == 0:
                            x_high(b + 1)
                        if s == 1:
                            values(b + 1, 1 - p)
                        if s == 2:
                            high(b + 1, 0)
                            high(b + 1, 1)
                        if s in (2, 3):
                            for k in range(4 * (s - 2), 4 * (s - 2) + 4):
                                stack(b + 1, 1 - p, k)
                        if s == 6:
                            max_row(b + 1, 0)
                    if s % 2 == 0 and s > 0:
                        outputs(b, s // 2 - 1)
                outputs(b, 3)
                if front:
                    max_row(b + 1, 1)

            def post(b):
                o_high(b)
                y_high(b)

            act.wait_ge(wqkv_in, 16)
            for c in range(C):
                copy(wqkv_h[:, c, :], wqkv_raw[:, c, :]).then_inc(wqkv_h_ok, 1)
            act.wait_ge(wp_in, 16)
            copy(wp_h[:, :, :], wp_raw).then_inc(wp_h_ok, 1)
            act.wait_ge(gw_in, 16)
            copy(gw_h[:, :, :], gw_raw[:, :, :]).then_inc(gw_h_ok, 1)
            x_high(0)
            act.wait_ge(filled, NT + 3)
            values(0, 0)
            high(0, 0)
            high(0, 1)
            for k in range(8):
                stack(0, 0, k)
            max_row(0, 0)
            max_row(0, 1)
            steps(act, step, post)

        @block.vector
        def _(dve):
            v = nc.vector

            def norm_stats(b, src, st, mv, stats, moments):
                for t in range(NT):
                    v.bn_stats(st[:, t, :], src(t)).then_inc(stats, 1)
                for t in range(NT):
                    wait_apart(dve, stats, b * NT + t + 1)
                    v.bn_aggr(mv[:, t, :], st[:, t, :]).then_inc(moments, 1)

            def normed(src, dst, mv, rs, done):
                for t in range(NT):
                    v.tensor_scalar(dst[:, t, :], src(t), mv[:, t, 0:1], rs[:, t:t + 1],
                                    ALU.subtract, ALU.mult).then_inc(done, 1)

            def f_norm_a(b):
                wait(dve, h_in, b + 1)
                norm_stats(b, lambda t: h0[:, b * NT + t, :], f_st, f_mv, f_stats, f_moments)

            def f_norm_b(b):
                wait(dve, f_rstd, b + 1)
                normed(lambda t: h0[:, b * NT + t, :], xn, f_mv, f_rs, f_normed)

            def x_low(b):
                wait(dve, xh_ok, b + 1)
                v.tensor_tensor(x_l[:, :, :, :].rearrange("p c t n -> p (c t n)"), f_bank[:, :],
                                x_h[:, :, :, :].rearrange("p c t n -> p (c t n)").bitcast(F32),
                                ALU.subtract).then_inc(xl_ok, 1)

            def rotate(b):
                for t in range(NT):
                    wait(dve, qk_ps, b * NT + t + 1)
                    src = s_bank[t][:, :].rearrange("p (h d) -> p h d", d=HD)
                    cos = rope_sb[:, t, 0:1, :].broadcast_to([P, 2 * NH, HD])
                    v.tensor_tensor(rope_a[:, t, :, :], src, cos, ALU.mult).then_inc(roped, 1)
                    swap = s_bank[t][:, :].rearrange("p (h i two) -> p h i two", two=2, i=HD // 2)[:, :, :, ::-1]
                    sin = rope_sb[:, t, 1:2, :].broadcast_to([P, 2 * NH, HD]).rearrange("p h (i two) -> p h i two", two=2)
                    v.tensor_tensor(rope_b[:, t, :, :].rearrange("p h (i two) -> p h i two", two=2), swap, sin,
                                    ALU.mult).then_inc(roped, 1)

            def rotated_sum(b, t):
                wait(dve, roped, b * 2 * NT + 2 * t + 2)
                v.tensor_tensor(qk[:, t, :, :], rope_a[:, t, :, :], rope_b[:, t, :, :], ALU.add).then_inc(rotated, 1)

            def low(b, t):
                wait(dve, part_h, b * NT + t + 1)
                for kind, a in ((0, 1), (1, 2)):
                    hs = slice(kind * NH, (kind + 1) * NH)
                    v.tensor_tensor(parts[:, t, hs, a, :], qk[:, t, hs, :], parts[:, t, hs, 0, :].bitcast(F32),
                                    ALU.subtract).then_inc(part_l, 1)

            def maximum(b, h):
                wait(dve, s_ps, b * NH + h + 1)
                pair = h // 2
                v.tensor_reduce(neg_max[:, pair // HALF, :, h % 2, pair % HALF],
                                s_bank[h % 2][:, :].rearrange("p (t n) -> p t n", t=NT), AX.X, ALU.max,
                                negate=True).then_inc(max_ok, 1)

            def max_split(b, u):
                wait(dve, max_ok, b * NH + 8 * u + 8)
                v.tensor_copy(max_parts[:, u, :, :, 0, :], neg_max[:, u, :, :, :]).then_inc(mh_ok, 1)
                wait(dve, mh_ok, b * 2 + u + 1)
                v.tensor_tensor(max_parts[:, u, :, :, 1, :], neg_max[:, u, :, :, :],
                                max_parts[:, u, :, :, 0, :].bitcast(F32), ALU.subtract).then_inc(ml_ok, 1)

            def o_norm(b):
                for t in range(NT):
                    wait(dve, ot_ps, b * NT + t + 1)
                    v.reciprocal(o_rs[:, t, :],
                                 m_bank[t][:, :].rearrange("p (h s) -> p h s", s=STRIP)[:, :, HD]).then_inc(ors_ok, 1)
                for t in range(NT):
                    wait(dve, ors_ok, b * NT + t + 1)
                    v.tensor_tensor(o_n[:, t, :, :], m_bank[t][:, :].rearrange("p (h s) -> p h s", s=STRIP)[:, :, 0:HD],
                                    o_rs[:, t, :].rearrange("p (h o) -> p h o", o=1).broadcast_to([P, NH, HD]),
                                    ALU.mult).then_inc(on_ok, 1)

            def o_low(b):
                wait(dve, oh_ok, b + 1)
                v.tensor_tensor(o_l[:, :, :, :].rearrange("p c t n -> p (c t n)"), m_bank[0][:, :],
                                o_h[:, :, :, :].rearrange("p c t n -> p (c t n)").bitcast(F32),
                                ALU.subtract).then_inc(ol_ok, 1)

            def residual(b):
                wait(dve, proj_ps, b + 1)
                for t in range(NT):
                    v.tensor_tensor(h1[:, t, :], m_bank[1][:, t * D:(t + 1) * D], h0[:, b * NT + t, :],
                                    ALU.add).then_inc(h1_ok, 1)
                wait(dve, h1_ok, b * NT + NT)
                norm_stats(b, lambda t: h1[:, t, :], g_st, g_mv, g_stats, g_moments)

            def g_norm_b(b):
                wait(dve, g_rstd, b + 1)
                normed(lambda t: h1[:, t, :], yn, g_mv, g_rs, g_normed)

            def y_low(b):
                wait(dve, yh_ok, b + 1)
                v.tensor_tensor(y_l[:, :, :, :].rearrange("p c t n -> p (c t n)"), m_bank[0][:, :],
                                y_h[:, :, :, :].rearrange("p c t n -> p (c t n)").bitcast(F32),
                                ALU.subtract).then_inc(yl_ok, 1)

            def choose(b):
                wait(dve, gate_ps, b + 1)
                v.tensor_copy(score[:, :, :], m_bank[1][:, 0:NT * N_EXP].rearrange("p (t e) -> p t e", t=NT)).then_inc(score_ok, 1)
                wait_apart(dve, score_ok, b + 1)
                for t in range(NT):
                    v.max(top[:, t, :], score[:, t, :]).then_inc(top_ok, 1)
                for t in range(NT):
                    wait_apart(dve, top_ok, b * NT + t + 1)
                    v.max_index(top_at[:, t, :], top[:, t, :], score[:, t, :]).then_inc(at_ok, 1)
                for t in range(NT):
                    wait(dve, at_ok, b * NT + t + 1)
                    v.tensor_scalar(mask[:, t, :], ramp_sb[:, :], top_at[:, t, 0:1], None, ALU.is_equal).then_inc(mask_ok, 1)

            def select(b, n):
                u, t = n // NT, n % NT
                wait(dve, exp_ps, b * 8 + n + 1)
                if n == 0:
                    wait(dve, mask_ok, b * NT + NT)
                    wait(dve, base_ok, b + 1)
                    wait(dve, res_ok, b)
                for j in range(2):
                    e = 2 * u + j
                    y = m_bank[t][:, j * D:(j + 1) * D]
                    if u == 0 and j == 1:
                        v.tensor_scalar(acc[:, 1, t, :], y, mask[:, t, e:e + 1], None, ALU.mult).then_inc(acc_ok, 1)
                        continue
                    if u > 0:
                        wait(dve, acc_ok, b * 16 + 2 * (n - 2) + j + 1)
                    v.scalar_tensor_tensor(out=acc[:, j, t, :], in0=y, scalar=mask[:, t, e:e + 1],
                                           in1=base[:, t, :] if u == 0 else acc[:, j, t, :],
                                           op0=ALU.mult, op1=ALU.add).then_inc(acc_ok, 1)

            def step(b, front, last, p=None):
                for s in range(8):
                    if last:
                        if s == 0:
                            o_norm(b - 1)
                        if s == 1:
                            o_low(b - 1)
                        if s == 2:
                            residual(b - 1)
                        if s == 3:
                            g_norm_b(b - 1)
                            y_low(b - 1)
                        if s == 4:
                            choose(b - 1)
                        if s >= 5:
                            for n in range(*((0, 2), (2, 5), (5, 8))[s - 5]):
                                select(b - 1, n)
                    if front:
                        if s == 0:
                            f_norm_a(b + 1)
                            f_norm_b(b + 1)
                            x_low(b + 1)
                        if s == 1:
                            rotate(b + 1)
                            rotated_sum(b + 1, 0)
                            rotated_sum(b + 1, 1)
                        if s == 2:
                            low(b + 1, 0)
                            low(b + 1, 1)
                        if s >= 4:
                            for h in range(4 * (s - 4), 4 * (s - 4) + 4):
                                maximum(b + 1, h)
                            if s == 5:
                                max_split(b + 1, 0)
                            if s == 7:
                                max_split(b + 1, 1)

            def post(b):
                o_norm(b)
                o_low(b)
                residual(b)
                g_norm_b(b)
                y_low(b)
                choose(b)
                for n in range(8):
                    select(b, n)

            for b in range(NB):
                v.memset(h0[:, b * NT:(b + 1) * NT, :], 0.0).then_inc(h_zero, 1)
            for t in range(NT):
                v.memset(parts[:, t, :, 3, :].bitcast(F32), 0.0).then_inc(filled, 1)
            for i in range(2):
                v.memset(vals[i][:, :, :, HD:STRIP], 0.0).then_inc(h_zero, 1)
            dve.wait_ge(filled, NT)
            dve.wait_ge(h_zero, NB + 2)
            v.memset(parts[:, :, NH:2 * NH, 3, 0:2].bitcast(F32), 1.0).then_inc(filled, 1)
            for i in range(2):
                v.memset(vals[i][:, :, :, HD:HD + 1], 1.0).then_inc(filled, 1)
            dve.wait_ge(ident_ok, 1)
            v.tensor_copy(ident_r[:, :], ident[:, :]).then_inc(identr_ok, 1)
            dve.wait_ge(wqkv_h_ok, C)
            for c in range(C):
                v.tensor_tensor(wqkv_l[:, c, :], wqkv_raw[:, c, :], wqkv_h[:, c, :].bitcast(F32),
                                ALU.subtract).then_inc(wqkv_l_ok, 1)
            dve.wait_ge(rope_in, 32)
            f_norm_a(0)
            f_norm_b(0)
            x_low(0)
            rotate(0)
            rotated_sum(0, 0)
            rotated_sum(0, 1)
            low(0, 0)
            low(0, 1)
            for h in range(NH):
                maximum(0, h)
                if h % 8 == 7:
                    max_split(0, h // 8)
            dve.wait_ge(wp_h_ok, 1)
            v.tensor_tensor(wp_l[:, :, :], wp_raw, wp_h[:, :, :].bitcast(F32), ALU.subtract).then_inc(wp_l_ok, 1)
            steps(dve, step, post)


def kernel(x, L0_tok_embeddings, L0_attn_w_qkv, L0_attn_w_proj, L0_ffn_gate_w, L0_ffn_expert_w):
    import concourse.bacc as bacc
    from concourse.bass_utils import run_bass_kernel_spmd

    def rows(a):
        a = a.reshape(-1, P, *a.shape[1:])
        return np.ascontiguousarray(a.swapaxes(0, 1))

    d = L0_tok_embeddings.shape[1]
    arrays = {
        "x": rows(np.asarray(x).reshape(-1)),
        "emb": np.ascontiguousarray(L0_tok_embeddings),
        "w_qkv": np.ascontiguousarray(L0_attn_w_qkv),
        "w_proj": np.ascontiguousarray(L0_attn_w_proj),
        "gate_w": rows(np.asarray(L0_ffn_gate_w).T),
        "expert_w": rows(np.asarray(L0_ffn_expert_w).transpose(2, 0, 1).reshape(d, -1)),
        "rope": rope_tables(x.shape[1], 16),
        "ramp": np.ascontiguousarray(np.broadcast_to(np.arange(N_EXP, dtype=np.float32), (P, N_EXP))),
    }
    nc = bacc.Bacc("TRN2", target_bir_lowering=False, num_devices=1)
    args = [nc.dram_tensor(f"in_{n}", a.shape, mybir.dt.from_np(a.dtype), kind="ExternalInput").ap()
            for n, a in arrays.items()]
    out = nc.dram_tensor("out", (*x.shape, d), F32, kind="ExternalOutput").ap()
    tower(nc, *args, out)
    r = run_bass_kernel_spmd(nc, [{f"in_{n}": a for n, a in arrays.items()}], core_ids=[0])
    return r.results[0]["out"]
```

```python
from contextlib import ExitStack

import numpy as np

import concourse.bass as bass
from concourse import mybir

F32 = mybir.dt.float32
F32R = mybir.dt.float32r
I32 = mybir.dt.int32
U32 = mybir.dt.uint32
ALU = mybir.AluOpType
ACT = mybir.ActivationFunctionType
AX = mybir.AxisListType

P = 128
EPS = 1e-5
RING = 8
STRIP = 32
N_EXP = 8


def rope_tables(n, hd):
    inv = (1.0 / np.float32(10000.0) ** (np.arange(0, hd, 2, dtype=np.float32) / np.float32(hd))).astype(np.float32)
    angle = np.arange(n, dtype=np.float32)[:, None] * inv[None, :]
    cos = np.repeat(np.cos(angle), 2, axis=-1)
    sin = np.repeat(np.sin(angle), 2, axis=-1)
    sin[:, 0::2] *= -1
    both = np.stack([cos, sin], axis=1).astype(np.float32)
    return np.ascontiguousarray(both.reshape(n // P, P, 2, hd).transpose(1, 0, 2, 3))


def tower(nc, x, emb, w_qkv, w_proj, gate_w, expert_w, rope, ramp, out):
    NB, N, _ = out.shape
    V, D = emb.shape
    HD = rope.shape[3]
    NH = D // HD
    NT = N // P
    C = D // P
    GROUPS = NH // 4
    SCALE = float(HD) ** -0.5
    KS = 3 * HD
    KM = KS + 2
    assert NT == 2 and C == 2 and NH == 16 and HD == 16 and NB % 2 == 0

    with ExitStack() as ctx:
        def sb(name, shape, dt=F32):
            return ctx.enter_context(nc.sbuf_tensor(name, shape, dt))

        def bank(name):
            return ctx.enter_context(nc.psum_tensor(name, [P, 512], F32))

        def sem(name):
            return ctx.enter_context(nc.semaphore(name))

        rope_sb = sb("rope_sb", [P, NT, 2, HD])
        ramp_sb = sb("ramp_sb", [P, N_EXP])
        ident = sb("ident", [P, P])
        ident_r = sb("ident_r", [P, P], F32R)
        neg_half = sb("neg_half", [P, NT])
        wqkv_h = sb("wqkv_h", [P, C, 3 * D], F32R)
        wqkv_l = sb("wqkv_l", [P, C, 3 * D], F32R)
        wp_h = sb("wp_h", [P, C, D], F32R)
        wp_l = sb("wp_l", [P, C, D], F32R)
        ew_raw = sb("ew_raw", [P, C, N_EXP * D])
        ew_h = sb("ew_h", [P, C, N_EXP * D], F32R)
        ew_l = sb("ew_l", [P, C, N_EXP * D], F32R)
        gw_raw = sb("gw_raw", [P, C, N_EXP])
        gw_h = sb("gw_h", [P, C, N_EXP], F32R)
        gw_l = sb("gw_l", [P, C, N_EXP], F32R)
        ids = sb("ids", [P, NB * NT], I32)
        h0 = sb("h0", [P, NB * NT, D])
        f_st = sb("f_st", [P, NT, 6])
        f_mv = sb("f_mv", [P, NT, 2])
        f_ve = sb("f_ve", [P, NT])
        f_rs = sb("f_rs", [P, NT])
        xn = sb("xn", [P, NT, D])
        x_h = sb("x_h", [P, C, NT, P], F32R)
        x_l = sb("x_l", [P, C, NT, P], F32R)
        rope_a = sb("rope_a", [P, NT, 2 * NH, HD])
        rope_b = sb("rope_b", [P, NT, 2 * NH, HD])
        qk = sb("qk", [P, NT, 4, HD, 8])
        qk_h = sb("qk_h", [P, 4, N], F32R)
        qk_l = sb("qk_l", [P, 4, N], F32R)
        q_stack = [sb(f"q_stack{i}", [P, 8, N], F32R) for i in range(2)]
        k_stack = [sb(f"k_stack{i}", [P, 8, N], F32R) for i in range(2)]
        vals = [sb(f"vals{i}", [P, NT, NH, STRIP]) for i in range(2)]
        neg_max = sb("neg_max", [P, 2, NT, 8])
        max_parts = sb("max_parts", [P, 2, NT, 2, 8], F32R)
        max_rows = sb("max_rows", [16, 2, N], F32R)
        probs = sb("probs", [P, RING, NT, N])
        wqkv_raw = probs[:, 0:3, :, :].rearrange("p r t n -> p (r t n)").rearrange("p (c n) -> p c n", c=C)
        wp_raw = probs[:, 3, :, :]
        o_t = sb("o_t", [P, GROUPS, N])
        o_rs = sb("o_rs", [P, NT, NH])
        o_n = sb("o_n", [P, NT, NH, HD])
        o_h = sb("o_h", [P, C, NT, P], F32R)
        o_l = sb("o_l", [P, C, NT, P], F32R)
        h1 = sb("h1", [P, NT, D])
        g_st = sb("g_st", [P, NT, 6])
        g_mv = sb("g_mv", [P, NT, 2])
        g_ve = sb("g_ve", [P, NT])
        g_rs = sb("g_rs", [P, NT])
        yn = sb("yn", [P, NT, D])
        y_h = [sb(f"y_h{i}", [P, C, NT, P], F32R) for i in range(2)]
        y_l = [sb(f"y_l{i}", [P, C, NT, P], F32R) for i in range(2)]
        base = sb("base", [P, NT, D])
        score = sb("score", [P, NT, N_EXP])
        top = sb("top", [P, NT, 8])
        top_at = sb("top_at", [P, NT, 8], U32)
        mask = sb("mask", [P, 2, NT, N_EXP])
        acc = sb("acc", [P, 2, NT, D])
        res = sb("res", [P, NT, D])

        s_bank = [bank("s_bank0"), bank("s_bank1")]
        f_bank = bank("f_bank")
        t_bank = [bank("t_bank0"), bank("t_bank1")]
        o_bank = bank("o_bank")
        m_bank = bank("m_bank")
        e_bank = bank("e_bank")

        ids_in, rope_in, wqkv_in, wp_in, ew_in, gw_in = map(sem, "ids_in rope_in wqkv_in wp_in ew_in gw_in".split())
        gathered = [sem(f"gathered{b}") for b in range(NB)]
        h_in = sem("h_in")
        h_zero, filled, pool_filled, ident_ok, identr_ok = map(sem, "h_zero filled pool_filled ident_ok identr_ok".split())
        wqkv_h_ok, wqkv_l_ok, wp_h_ok, wp_l_ok = map(sem, "wqkv_h_ok wqkv_l_ok wp_h_ok wp_l_ok".split())
        ew_h_ok, ew_l_ok, gw_h_ok, gw_l_ok = map(sem, "ew_h_ok ew_l_ok gw_h_ok gw_l_ok".split())
        f_stats, f_moments, f_var, f_rstd, f_normed = map(sem, "f_stats f_moments f_var f_rstd f_normed".split())
        xt_ps, xh_ok, xl_ok, v_ps, v_ok, qk_ps = map(sem, "xt_ps xh_ok xl_ok v_ps v_ok qk_ps".split())
        roped, rotated, qkt_ps, qkh_ok, qkl_ok, ones_ok = map(
            sem, "roped rotated qkt_ps qkh_ok qkl_ok ones_ok".split())
        stack_in = [sem("stack_in0"), sem("stack_in1")]
        s_ps, max_ok, mh_ok, ml_ok, mt_ps, mt_ok = map(sem, "s_ps max_ok mh_ok ml_ok mt_ps mt_ok".split())
        m_in = [sem("m_in0"), sem("m_in1")]
        t_ps, exp_ok, o_ps, o_ok = map(sem, "t_ps exp_ok o_ps o_ok".split())
        ot_ps, ors_ok, on_ok, ont_ps, oh_ok, ol_ok, proj_ps, h1_ok = map(
            sem, "ot_ps ors_ok on_ok ont_ps oh_ok ol_ok proj_ps h1_ok".split())
        g_stats, g_moments, g_var, g_rstd, g_normed, base_ok = map(
            sem, "g_stats g_moments g_var g_rstd g_normed base_ok".split())
        yt_ps, yh_ok, yl_ok, gate_ps, score_ok, top_ok, at_ok, mask_ok = map(
            sem, "yt_ps yh_ok yl_ok gate_ps score_ok top_ok at_ok mask_ok".split())
        exp_ps, acc_ok, res_ok, out_ok = map(sem, "expert_ps acc_ok res_ok out_ok".split())

        def here(b, k):
            return not isinstance(b, int) or 0 <= b + k < NB

        def steps(engine, step):
            for b in range(-2, 2):
                step(b, b % 2)
            with engine.Fori(0, (NB - 4) // 2) as i:
                step(i * 2 + 2, 0)
                step(i * 2 + 3, 1)
            for b in range(NB - 2, NB + 2):
                step(b, b % 2)

        UNITS = 8

        def place(h):
            return 64 * (h // 8), h % 8

        def expert_banks(b):
            return [e_bank] + s_bank if isinstance(b, int) and b >= NB - 2 else [e_bank]

        def wait(engine, semaphore, value):
            if not isinstance(value, int) or value > 0:
                engine.wait_ge(semaphore, value)

        def wait_apart(engine, semaphore, value):
            if not isinstance(value, int):
                value = engine.snap(engine.to_reg(value))
            engine.wait_ge(ident_ok, 1)
            wait(engine, semaphore, value)

        block = ctx.enter_context(nc.Block())

        @block.sync
        def _(sp):
            sp.sem_inc(out_ok, 16)
            sp.dma_start(ids[:, :], x).then_inc(ids_in, 16)
            sp.dma_start(wqkv_raw, w_qkv.rearrange("(c p) n -> p c n", p=P)).then_inc(wqkv_in, 16)
            sp.dma_start(rope_sb[:, :, :, :], rope).then_inc(rope_in, 16)
            sp.dma_start(ramp_sb[:, :], ramp).then_inc(rope_in, 16)
            sp.dma_start(wp_raw, w_proj.rearrange("(c p) n -> p c n", p=P)).then_inc(wp_in, 16)
            sp.dma_start(gw_raw[:, :, :], gate_w).then_inc(gw_in, 16)
            sp.dma_start(ew_raw[:, :, :], expert_w).then_inc(ew_in, 16)

            def landed(b):
                sp.wait_ge(gathered[b], 16 * NT)
                sp.sem_inc(h_in, 1)

            def maximum(b, p, u):
                wait(sp, mt_ok, b * 2 + u + 1)
                r = 64 * u + KS
                sp.dma_start(q_stack[p][r:r + 2, :, :].bitcast(F32), max_rows[:, u, :].bitcast(F32)).then_inc(m_in[u], 16)

            def restack(b, p, half):
                taken = (b - 2) * NH + 8 * half + 8
                if not isinstance(b, int):
                    taken = sp.snap(sp.to_reg(taken))
                wait(sp, qkl_ok, b * NT + NT)
                wait(sp, t_ps, taken)
                for stack, group, blocks in ((q_stack[p], half, (qk_h, qk_l, qk_h)),
                                             (k_stack[p], 2 + half, (qk_h, qk_h, qk_l))):
                    for i, part in enumerate(blocks):
                        r = 64 * half + i * HD
                        sp.dma_start(stack[r:r + HD, :, :].bitcast(F32),
                                     part[:, group, :].bitcast(F32)).then_inc(stack_in[half], 16)

            def store(b):
                wait(sp, res_ok, b + 2)
                sp.dma_start(out[b].rearrange("(t p) d -> p t d", p=P), res[:, :, :]).then_inc(out_ok, 16)

            def step(b, p):
                if here(b, 0):
                    maximum(b, p, 1)
                if here(b, 2):
                    restack(b + 2, p, 0)
                if here(b, 1):
                    maximum(b + 1, 1 - p, 0)
                if here(b, 2):
                    restack(b + 2, p, 1)
                if here(b, -2):
                    store(b - 2)

            for b in range(NB):
                landed(b)
            sp.wait_ge(ones_ok, 4)
            steps(sp, step)
            sp.wait_ge(out_ok, 16 * (NB + 1))

        @block.gpsimd
        def _(pool):
            g = nc.gpsimd
            pool.sem_inc(res_ok, 1)
            g.memset(ident[:, :], 0.0).then_inc(pool_filled, 1)
            g.memset(neg_half[:, :], -0.5).then_inc(pool_filled, 1)
            pool.wait_ge(pool_filled, 2)
            g.affine_select(out=ident[:, :], in_=ident[:, :], compare_op=ALU.not_equal, fill=1.0, base=0,
                            pattern=[[-1, P]], channel_multiplier=1).then_inc(ident_ok, 1)
            pool.wait_ge(ids_in, 16)
            for j in range(NB * NT):
                pool.wait_ge(h_zero, j // NT + 1)
                g.indirect_dma_start(h0[:, j, :], None, emb, bass.IndirectOffsetOnAxis(ap=ids[:, j:j + 1], axis=0),
                                     bounds_check=V - 1, oob_is_err=False).then_inc(gathered[j // NT], 16)

            def f_rs_of(b):
                wait_apart(pool, f_moments, b * NT + NT)
                g.tensor_scalar(f_ve[:, :], f_mv[:, :, 1], EPS, None, ALU.add).then_inc(f_var, 1)
                wait(pool, f_var, b + 1)
                g.tensor_tensor(f_rs[:, :], f_ve[:, :], neg_half[:, :], ALU.pow).then_inc(f_rstd, 1)

            def rotated_sum(b, t):
                wait(pool, roped, b * 2 * NT + 2 * t + 2)
                g.tensor_tensor(qk[:, t, :, :, :].rearrange("p g d j -> p g j d"),
                                rope_a[:, t, :, :].rearrange("p (g j) d -> p g j d", j=8),
                                rope_b[:, t, :, :].rearrange("p (g j) d -> p g j d", j=8),
                                ALU.add).then_inc(rotated, 1)

            def g_rs_of(b):
                wait_apart(pool, g_moments, b * NT + NT)
                g.tensor_scalar(g_ve[:, :], g_mv[:, :, 1], EPS, None, ALU.add).then_inc(g_var, 1)
                wait(pool, g_var, b + 1)
                g.tensor_tensor(g_rs[:, :], g_ve[:, :], neg_half[:, :], ALU.pow).then_inc(g_rstd, 1)

            def residuals(b):
                wait(pool, g_normed, b * NT + NT)
                g.tensor_tensor(base[:, :, :], h1[:, :, :], yn[:, :, :], ALU.add).then_inc(base_ok, 1)

            def finish(b):
                wait(pool, acc_ok, b * 16 + 17)
                wait(pool, out_ok, b * 16 + 16)
                g.tensor_tensor(res[:, :, :], acc[:, 0, :, :], acc[:, 1, :, :], ALU.add).then_inc(res_ok, 1)

            def expert_weights():
                for k in range(8):
                    pool.wait_ge(ew_h_ok, k + 1)
                    w = slice(k % 4 * 2 * D, (k % 4 + 1) * 2 * D)
                    g.tensor_tensor(ew_l[:, k // 4, w], ew_raw[:, k // 4, w], ew_h[:, k // 4, w].bitcast(F32),
                                    ALU.subtract).then_inc(ew_l_ok, 1)

            def step(b, p):
                if here(b, 2):
                    f_rs_of(b + 2)
                if here(b, 2):
                    rotated_sum(b + 2, 0)
                    rotated_sum(b + 2, 1)
                if here(b, -1):
                    g_rs_of(b - 1)
                    residuals(b - 1)
                if here(b, -2):
                    finish(b - 2)
                if isinstance(b, int) and b == 0:
                    expert_weights()

            pool.wait_ge(gw_h_ok, 1)
            g.tensor_tensor(gw_l[:, :, :], gw_raw[:, :, :], gw_h[:, :, :].bitcast(F32), ALU.subtract).then_inc(gw_l_ok, 1)
            steps(pool, step)

        @block.tensor
        def _(pe):
            mm = nc.tensor.matmul
            tr = nc.tensor.transpose

            def product(o, xh, xl, wh, wl):
                n = 0
                for c in range(C):
                    for a, w in ((xh, wh), (xl, wh), (xh, wl)):
                        m = mm(o, a(c), w(c), start=(n == 0), stop=(n == 3 * C - 1))
                        n += 1
                return m

            def x_transpose(b):
                wait(pe, v_ok, b)
                wait(pe, f_normed, b * NT + NT)
                for c in range(C):
                    for t in range(NT):
                        k = (c * NT + t) * P
                        m = tr(f_bank[:, k:k + P], xn[:, t, c * P:(c + 1) * P], ident[:, :])
                m.then_inc(xt_ps, 1)

            def project_v(b):
                wait(pe, mt_ok, b * 2)
                for t in range(NT):
                    m = product(f_bank[:, t * D:(t + 1) * D], lambda c: x_h[:, c, t, :], lambda c: x_l[:, c, t, :],
                                lambda c: wqkv_h[:, c, 2 * D:3 * D], lambda c: wqkv_l[:, c, 2 * D:3 * D])
                m.then_inc(v_ps, 1)

            def project_qk(b, t):
                if t == 0:
                    wait(pe, xl_ok, b + 1)
                else:
                    wait(pe, roped, b * 2 * NT + 2)
                product(f_bank[:, :], lambda c: x_h[:, c, t, :], lambda c: x_l[:, c, t, :],
                        lambda c: wqkv_h[:, c, 0:2 * D], lambda c: wqkv_l[:, c, 0:2 * D]).then_inc(qk_ps, 1)

            def qk_transpose(b, t):
                if t == 0:
                    wait(pe, roped, b * 2 * NT + 2 * NT)
                else:
                    wait(pe, qkh_ok, b * NT + 1)
                    wait(pe, qkl_ok, b * NT + 1)
                wait(pe, rotated, b * NT + t + 1)
                for i in range(4):
                    m = tr(f_bank[:, i * P:(i + 1) * P], qk[:, t, i, :, :].rearrange("p d j -> p (d j)"),
                           ident[:, :])
                m.then_inc(qkt_ps, 1)

            def scores(b, p, h):
                if h % 8 == 0:
                    wait(pe, stack_in[h // 8], b * 96 + 96)
                wait(pe, max_ok, b * NH + h - 1)
                r, pair = place(h)
                for t in range(NT):
                    m = mm(s_bank[h % 2][:, t * N:(t + 1) * N], q_stack[p][r:r + KS, pair, t * P:(t + 1) * P],
                           k_stack[p][r:r + KS, pair, :], start=True, stop=True)
                m.then_inc(s_ps, 1)

            def max_transpose(b, u):
                if u == 1:
                    wait(pe, mt_ok, b * 2 + 1)
                elif here(b, 1):
                    wait(pe, qkh_ok, (b + 1) * NT + NT)
                    wait(pe, qkl_ok, (b + 1) * NT + NT)
                else:
                    wait(pe, v_ok, b + 1)
                wait(pe, ml_ok, b * 2 + u + 1)
                for t in range(NT):
                    m = tr(f_bank[0:16, t * P:(t + 1) * P].bitcast(F32R),
                           max_parts[:, u, t, :, :].rearrange("p a b -> p (a b)"), ident_r[:, :])
                m.then_inc(mt_ps, 1)

            def t_scores(b, p, h):
                if h % 8 == 0:
                    wait(pe, m_in[h // 8], b * 16 + 16)
                wait(pe, exp_ok, b * NH + h - 1)
                r, pair = place(h)
                for c in range(NT):
                    m = mm(t_bank[h % 2][:, c * N:(c + 1) * N], k_stack[p][r:r + KM, pair, c * P:(c + 1) * P],
                           q_stack[p][r:r + KM, pair, :], start=True, stop=True)
                m.then_inc(t_ps, 1)

            def outputs(b, p, g):
                wait(pe, exp_ok, b * NH + 4 * g + 4)
                wait(pe, o_ok, b * GROUPS + g)
                for c in range(NT):
                    for j in range(4):
                        m = mm(o_bank[STRIP * j:STRIP * (j + 1), 0:N], vals[p][:, c, 4 * g + j, :],
                               probs[:, (4 * g + j) % RING, c, :], start=(c == 0), stop=(c == NT - 1),
                               skip_group_check=True)
                m.then_inc(o_ps, 1)

            def o_transpose(b, t):
                if t == 0:
                    wait(pe, o_ok, b * GROUPS + GROUPS)
                    wait(pe, score_ok, b)
                else:
                    wait(pe, on_ok, b * NT + 1)
                for g in range(GROUPS):
                    m = tr(m_bank[:, g * P:(g + 1) * P], o_t[:, g, t * P:(t + 1) * P], ident[:, :])
                m.then_inc(ot_ps, 1)

            def on_transpose(b):
                wait(pe, on_ok, b * NT + NT)
                for c in range(C):
                    for t in range(NT):
                        k = (c * NT + t) * P
                        m = tr(m_bank[:, k:k + P],
                               o_n[:, t, c * NH // C:(c + 1) * NH // C, :].rearrange("p h d -> p (h d)"), ident[:, :])
                m.then_inc(ont_ps, 1)

            def out_project(b):
                wait(pe, ol_ok, b + 1)
                for t in range(NT):
                    m = product(m_bank[:, t * D:(t + 1) * D], lambda c: o_h[:, c, t, :], lambda c: o_l[:, c, t, :],
                                lambda c: wp_h[:, c, :], lambda c: wp_l[:, c, :])
                m.then_inc(proj_ps, 1)

            def y_transpose(b):
                wait(pe, g_normed, b * NT + NT)
                for c in range(C):
                    for t in range(NT):
                        k = (c * NT + t) * P
                        m = tr(m_bank[:, k:k + P], yn[:, t, c * P:(c + 1) * P], ident[:, :])
                m.then_inc(yt_ps, 1)

            def gate(b, p):
                wait(pe, yl_ok, b + 1)
                for t in range(NT):
                    m = product(m_bank[:, t * N_EXP:(t + 1) * N_EXP], lambda c: y_h[p][:, c, t, :],
                                lambda c: y_l[p][:, c, t, :], lambda c: gw_h[:, c, :], lambda c: gw_l[:, c, :])
                m.then_inc(gate_ps, 1)

            def experts(b, p, n, banks):
                u, t = n // NT, n % NT
                if n == 0 and isinstance(b, int) and b == 0:
                    pe.wait_ge(ew_l_ok, 8)
                wait(pe, acc_ok, b * 16 + 2 * max(n - len(banks) + 1, 0) + 1)
                product(banks[n % len(banks)][:, :], lambda c: y_h[p][:, c, t, :], lambda c: y_l[p][:, c, t, :],
                        lambda c: ew_h[:, c, 2 * u * D:2 * (u + 1) * D],
                        lambda c: ew_l[:, c, 2 * u * D:2 * (u + 1) * D]).then_inc(exp_ps, 1)

            def step(b, p):
                for s in range(NH):
                    if here(b, 0):
                        t_scores(b, p, s)
                    if here(b, 1):
                        scores(b + 1, 1 - p, s)
                    if here(b, 0) and s == 1:
                        max_transpose(b, 1)
                    if here(b, 1) and s == 2:
                        project_v(b + 1)
                    if here(b, 1) and s == 13:
                        max_transpose(b + 1, 0)
                    if here(b, -1):
                        if s in (3, 5):
                            o_transpose(b - 1, (s - 3) // 2)
                        if s == 7:
                            on_transpose(b - 1)
                        if s == 13:
                            y_transpose(b - 1)
                        if s == 15:
                            gate(b - 1, 1 - p)
                    if here(b, 2):
                        if s == 3:
                            x_transpose(b + 2)
                        if s in (5, 7):
                            project_qk(b + 2, (s - 5) // 2)
                        if s in (9, 11):
                            qk_transpose(b + 2, (s - 9) // 2)
                    if here(b, -1) and s == 1:
                        outputs(b - 1, 1 - p, 3)
                    if here(b, 0) and s in (5, 9, 13):
                        outputs(b, p, (s - 5) // 4)
                    if here(b, -1) and s == 9:
                        out_project(b - 1)
                    if here(b, -2) and s % 2 == 0:
                        experts(b - 2, p, s // 2, expert_banks(b - 2))

            pe.wait_ge(ident_ok, 1)
            pe.wait_ge(identr_ok, 1)
            pe.wait_ge(filled, 2)
            pe.wait_ge(wqkv_l_ok, C)
            pe.wait_ge(wp_l_ok, 1)
            pe.wait_ge(gw_l_ok, 1)
            steps(pe, step)

        @block.scalar
        def _(act):
            def copy(o, i):
                return nc.scalar.activation(o, i, ACT.Copy)

            def x_high(b):
                wait(act, xt_ps, b + 1)
                copy(x_h[:, :, :, :].rearrange("p c t n -> p (c t n)"), f_bank[:, :]).then_inc(xh_ok, 1)

            def values(b, p):
                wait(act, v_ps, b + 1)
                copy(vals[p][:, :, :, 0:HD], f_bank[:, :].rearrange("p (t h d) -> p t h d", t=NT, h=NH)).then_inc(v_ok, 1)

            def qk_high(b, t):
                wait(act, qkt_ps, b * NT + t + 1)
                for half in range(2):
                    wait(act, stack_in[half], b * 96)
                copy(qk_h[:, :, t * P:(t + 1) * P],
                     f_bank[:, :].rearrange("p (g n) -> p g n", g=4)).then_inc(qkh_ok, 1)

            def max_row(b, u):
                wait(act, mt_ps, b * 2 + u + 1)
                copy(max_rows[:, u, :], f_bank[0:16, 0:N]).then_inc(mt_ok, 1)

            def exp(b, h):
                wait(act, t_ps, b * NH + h + 1)
                if h % 4 == 0:
                    wait(act, o_ps, b * GROUPS + h // 4 - 1)
                nc.scalar.activation(probs[:, h % RING, :, :].rearrange("p c n -> p (c n)"), t_bank[h % 2][:, :],
                                     ACT.Exp, scale=SCALE).then_inc(exp_ok, 1)

            def outputs(b, g):
                wait(act, o_ps, b * GROUPS + g + 1)
                if g == 0:
                    wait(act, ot_ps, b * NT)
                copy(o_t[:, g, :], o_bank[:, 0:N]).then_inc(o_ok, 1)

            def o_high(b):
                wait(act, ont_ps, b + 1)
                copy(o_h[:, :, :, :].rearrange("p c t n -> p (c t n)"), m_bank[:, :]).then_inc(oh_ok, 1)

            def y_high(b, p):
                wait(act, yt_ps, b + 1)
                copy(y_h[p][:, :, :, :].rearrange("p c t n -> p (c t n)"), m_bank[:, :]).then_inc(yh_ok, 1)

            def expert_weights(k):
                if k == 0:
                    act.wait_ge(ew_in, 16)
                w = slice(k % 4 * 2 * D, (k % 4 + 1) * 2 * D)
                copy(ew_h[:, k // 4, w], ew_raw[:, k // 4, w]).then_inc(ew_h_ok, 1)

            def step(b, p):
                for s in range(NH):
                    if here(b, 0):
                        exp(b, s)
                    if here(b, 0) and s == 1:
                        max_row(b, 1)
                    if here(b, 1) and s == 2:
                        values(b + 1, 1 - p)
                    if here(b, -1) and s == 2:
                        outputs(b - 1, 3)
                    if here(b, 2) and s == 3:
                        x_high(b + 2)
                    if here(b, 0) and s in (6, 10, 14):
                        outputs(b, (s - 6) // 4)
                    if here(b, -1) and s == 7:
                        o_high(b - 1)
                    if here(b, 2) and s in (9, 11):
                        qk_high(b + 2, (s - 9) // 2)
                    if here(b, 1) and s == 13:
                        max_row(b + 1, 0)
                    if here(b, -1) and s == 13:
                        y_high(b - 1, 1 - p)
                    if isinstance(b, int) and b == 0 and s % 2:
                        expert_weights(s // 2)

            act.wait_ge(wqkv_in, 16)
            for c in range(C):
                copy(wqkv_h[:, c, :], wqkv_raw[:, c, :]).then_inc(wqkv_h_ok, 1)
            act.wait_ge(wp_in, 16)
            copy(wp_h[:, :, :], wp_raw).then_inc(wp_h_ok, 1)
            act.wait_ge(gw_in, 16)
            copy(gw_h[:, :, :], gw_raw[:, :, :]).then_inc(gw_h_ok, 1)
            act.wait_ge(filled, 2)
            steps(act, step)

        @block.vector
        def _(dve):
            v = nc.vector

            def norm_stats(b, src, st, mv, stats, moments):
                for t in range(NT):
                    v.bn_stats(st[:, t, :], src(t)).then_inc(stats, 1)
                for t in range(NT):
                    wait_apart(dve, stats, b * NT + t + 1)
                    v.bn_aggr(mv[:, t, :], st[:, t, :]).then_inc(moments, 1)

            def normed(src, dst, mv, rs, done):
                for t in range(NT):
                    v.tensor_scalar(dst[:, t, :], src(t), mv[:, t, 0:1], rs[:, t:t + 1],
                                    ALU.subtract, ALU.mult).then_inc(done, 1)

            def f_norm_a(b):
                wait(dve, h_in, b + 1)
                norm_stats(b, lambda t: h0[:, b * NT + t, :], f_st, f_mv, f_stats, f_moments)

            def f_norm_b(b):
                wait(dve, f_rstd, b + 1)
                normed(lambda t: h0[:, b * NT + t, :], xn, f_mv, f_rs, f_normed)

            def x_low(b):
                wait(dve, xh_ok, b + 1)
                v.tensor_tensor(x_l[:, :, :, :].rearrange("p c t n -> p (c t n)"), f_bank[:, :],
                                x_h[:, :, :, :].rearrange("p c t n -> p (c t n)").bitcast(F32),
                                ALU.subtract).then_inc(xl_ok, 1)

            def rotate(b, t):
                wait(dve, qk_ps, b * NT + t + 1)
                src = f_bank[:, :].rearrange("p (h d) -> p h d", d=HD)
                cos = rope_sb[:, t, 0:1, :].broadcast_to([P, 2 * NH, HD])
                v.tensor_tensor(rope_a[:, t, :, :], src, cos, ALU.mult).then_inc(roped, 1)
                swap = f_bank[:, :].rearrange("p (h i two) -> p h i two", two=2, i=HD // 2)[:, :, :, ::-1]
                sin = rope_sb[:, t, 1:2, :].broadcast_to([P, 2 * NH, HD]).rearrange("p h (i two) -> p h i two", two=2)
                v.tensor_tensor(rope_b[:, t, :, :].rearrange("p h (i two) -> p h i two", two=2), swap, sin,
                                ALU.mult).then_inc(roped, 1)

            def qk_low(b, t):
                wait(dve, qkh_ok, b * NT + t + 1)
                v.tensor_tensor(qk_l[:, :, t * P:(t + 1) * P], f_bank[:, :].rearrange("p (g n) -> p g n", g=4),
                                qk_h[:, :, t * P:(t + 1) * P].bitcast(F32), ALU.subtract).then_inc(qkl_ok, 1)

            def maximum(b, h):
                wait(dve, s_ps, b * NH + h + 1)
                v.tensor_reduce(neg_max[:, h // 8, :, h % 8],
                                s_bank[h % 2][:, :].rearrange("p (t n) -> p t n", t=NT), AX.X, ALU.max,
                                negate=True).then_inc(max_ok, 1)

            def max_split(b, u):
                wait(dve, max_ok, b * NH + 8 * u + 8)
                v.tensor_copy(max_parts[:, u, :, 0, :], neg_max[:, u, :, :]).then_inc(mh_ok, 1)
                wait(dve, mh_ok, b * 2 + u + 1)
                v.tensor_tensor(max_parts[:, u, :, 1, :], neg_max[:, u, :, :],
                                max_parts[:, u, :, 0, :].bitcast(F32), ALU.subtract).then_inc(ml_ok, 1)

            def o_norm(b, t):
                wait(dve, ot_ps, b * NT + t + 1)
                o = m_bank[:, :].rearrange("p (h s) -> p h s", s=STRIP)
                v.reciprocal(o_rs[:, t, :], o[:, :, HD]).then_inc(ors_ok, 1)
                wait(dve, ors_ok, b * NT + t + 1)
                v.tensor_tensor(o_n[:, t, :, :], o[:, :, 0:HD],
                                o_rs[:, t, :].rearrange("p (h o) -> p h o", o=1).broadcast_to([P, NH, HD]),
                                ALU.mult).then_inc(on_ok, 1)

            def o_low(b):
                wait(dve, oh_ok, b + 1)
                v.tensor_tensor(o_l[:, :, :, :].rearrange("p c t n -> p (c t n)"), m_bank[:, :],
                                o_h[:, :, :, :].rearrange("p c t n -> p (c t n)").bitcast(F32),
                                ALU.subtract).then_inc(ol_ok, 1)

            def residual(b):
                wait(dve, proj_ps, b + 1)
                for t in range(NT):
                    v.tensor_tensor(h1[:, t, :], m_bank[:, t * D:(t + 1) * D], h0[:, b * NT + t, :],
                                    ALU.add).then_inc(h1_ok, 1)
                wait(dve, h1_ok, b * NT + NT)
                norm_stats(b, lambda t: h1[:, t, :], g_st, g_mv, g_stats, g_moments)

            def g_norm_b(b):
                wait(dve, g_rstd, b + 1)
                normed(lambda t: h1[:, t, :], yn, g_mv, g_rs, g_normed)

            def y_low(b, p):
                wait(dve, yh_ok, b + 1)
                v.tensor_tensor(y_l[p][:, :, :, :].rearrange("p c t n -> p (c t n)"), m_bank[:, :],
                                y_h[p][:, :, :, :].rearrange("p c t n -> p (c t n)").bitcast(F32),
                                ALU.subtract).then_inc(yl_ok, 1)

            def choose(b, p):
                wait(dve, gate_ps, b + 1)
                v.tensor_copy(score[:, :, :], m_bank[:, 0:NT * N_EXP].rearrange("p (t e) -> p t e", t=NT)).then_inc(score_ok, 1)
                wait_apart(dve, score_ok, b + 1)
                for t in range(NT):
                    v.max(top[:, t, :], score[:, t, :]).then_inc(top_ok, 1)
                for t in range(NT):
                    wait_apart(dve, top_ok, b * NT + t + 1)
                    v.max_index(top_at[:, t, :], top[:, t, :], score[:, t, :]).then_inc(at_ok, 1)
                for t in range(NT):
                    wait(dve, at_ok, b * NT + t + 1)
                    v.tensor_scalar(mask[:, p, t, :], ramp_sb[:, :], top_at[:, t, 0:1], None, ALU.is_equal).then_inc(mask_ok, 1)

            def select(b, p, n, banks):
                u, t = n // NT, n % NT
                wait(dve, exp_ps, b * 8 + n + 1)
                if n == 0:
                    wait(dve, mask_ok, b * NT + NT)
                    wait(dve, base_ok, b + 1)
                    wait(dve, res_ok, b + 1)
                for j in range(2):
                    e = 2 * u + j
                    y = banks[n % len(banks)][:, j * D:(j + 1) * D]
                    if u == 0 and j == 1:
                        v.tensor_scalar(acc[:, 1, t, :], y, mask[:, p, t, e:e + 1], None, ALU.mult).then_inc(acc_ok, 1)
                        continue
                    if u > 0:
                        wait(dve, acc_ok, b * 16 + 2 * (n - 2) + j + 2)
                    v.scalar_tensor_tensor(out=acc[:, j, t, :], in0=y, scalar=mask[:, p, t, e:e + 1],
                                           in1=base[:, t, :] if u == 0 else acc[:, j, t, :],
                                           op0=ALU.mult, op1=ALU.add).then_inc(acc_ok, 1)

            def step(b, p):
                for s in range(NH):
                    if s > 0 and here(b, 1):
                        maximum(b + 1, s - 1)
                    if s == 0 and here(b, 0):
                        maximum(b, NH - 1)
                        max_split(b, 1)
                    if here(b, -2) and s == 0:
                        choose(b - 2, p)
                    if here(b, -2) and s % 2:
                        select(b - 2, p, s // 2, expert_banks(b - 2))
                    if here(b, 2):
                        if s == 0:
                            f_norm_a(b + 2)
                        if s == 2:
                            f_norm_b(b + 2)
                        if s == 4:
                            x_low(b + 2)
                        if s in (6, 8):
                            rotate(b + 2, (s - 6) // 2)
                        if s in (10, 12):
                            qk_low(b + 2, (s - 10) // 2)
                    if here(b, -1):
                        if s in (4, 6):
                            o_norm(b - 1, (s - 4) // 2)
                        if s == 8:
                            o_low(b - 1)
                        if s == 10:
                            residual(b - 1)
                        if s == 11:
                            g_norm_b(b - 1)
                        if s == 14:
                            y_low(b - 1, 1 - p)
                    if s == 12 and here(b, 1):
                        max_split(b + 1, 0)

            dve.sem_inc(acc_ok, 1)
            for b in range(NB):
                v.memset(h0[:, b * NT:(b + 1) * NT, :], 0.0).then_inc(h_zero, 1)
            for i in range(2):
                v.memset(vals[i][:, :, :, HD:STRIP], 0.0).then_inc(h_zero, 1)
            dve.wait_ge(h_zero, NB + 2)
            for i in range(2):
                v.memset(vals[i][:, :, :, HD:HD + 1], 1.0).then_inc(filled, 1)
            dve.wait_ge(ident_ok, 1)
            v.tensor_copy(ident_r[:, :], ident[:, :]).then_inc(identr_ok, 1)
            dve.wait_ge(wqkv_h_ok, C)
            for c in range(C):
                v.tensor_tensor(wqkv_l[:, c, :], wqkv_raw[:, c, :], wqkv_h[:, c, :].bitcast(F32),
                                ALU.subtract).then_inc(wqkv_l_ok, 1)
            for i in range(2):
                for r in (32, 96):
                    v.memset(k_stack[i][r:r + 32, :, :].bitcast(F32), 1.0).then_inc(ones_ok, 1)
            dve.wait_ge(rope_in, 32)
            dve.wait_ge(wp_h_ok, 1)
            v.tensor_tensor(wp_l[:, :, :], wp_raw, wp_h[:, :, :].bitcast(F32), ALU.subtract).then_inc(wp_l_ok, 1)
            steps(dve, step)


def kernel(x, L0_tok_embeddings, L0_attn_w_qkv, L0_attn_w_proj, L0_ffn_gate_w, L0_ffn_expert_w):
    import concourse.bacc as bacc
    from concourse.bass_utils import run_bass_kernel_spmd

    def rows(a):
        a = a.reshape(-1, P, *a.shape[1:])
        return np.ascontiguousarray(a.swapaxes(0, 1))

    d = L0_tok_embeddings.shape[1]
    arrays = {
        "x": rows(np.asarray(x).reshape(-1)),
        "emb": np.ascontiguousarray(L0_tok_embeddings),
        "w_qkv": np.ascontiguousarray(L0_attn_w_qkv),
        "w_proj": np.ascontiguousarray(L0_attn_w_proj),
        "gate_w": rows(np.asarray(L0_ffn_gate_w).T),
        "expert_w": rows(np.asarray(L0_ffn_expert_w).transpose(2, 0, 1).reshape(d, -1)),
        "rope": rope_tables(x.shape[1], 16),
        "ramp": np.ascontiguousarray(np.broadcast_to(np.arange(N_EXP, dtype=np.float32), (P, N_EXP))),
    }
    nc = bacc.Bacc("TRN2", target_bir_lowering=False, num_devices=1)
    args = [nc.dram_tensor(f"in_{n}", a.shape, mybir.dt.from_np(a.dtype), kind="ExternalInput").ap()
            for n, a in arrays.items()]
    out = nc.dram_tensor("out", (*x.shape, d), F32, kind="ExternalOutput").ap()
    tower(nc, *args, out)
    r = run_bass_kernel_spmd(nc, [{f"in_{n}": a for n, a in arrays.items()}], core_ids=[0])
    return r.results[0]["out"]
```

```python
from contextlib import ExitStack

import numpy as np

import concourse.bass as bass
from concourse import mybir

F32 = mybir.dt.float32
F32R = mybir.dt.float32r
I32 = mybir.dt.int32
U32 = mybir.dt.uint32
ALU = mybir.AluOpType
ACT = mybir.ActivationFunctionType
AX = mybir.AxisListType

P = 128
EPS = 1e-5
RING = 8
STRIP = 32
N_EXP = 8


def rope_tables(n, hd):
    inv = (1.0 / np.float32(10000.0) ** (np.arange(0, hd, 2, dtype=np.float32) / np.float32(hd))).astype(np.float32)
    angle = np.arange(n, dtype=np.float32)[:, None] * inv[None, :]
    cos = np.repeat(np.cos(angle), 2, axis=-1)
    sin = np.repeat(np.sin(angle), 2, axis=-1)
    sin[:, 0::2] *= -1
    both = np.stack([cos, sin], axis=1).astype(np.float32)
    return np.ascontiguousarray(both.reshape(n // P, P, 2, hd).transpose(1, 0, 2, 3))


def tower(nc, x, emb, w_qkv, w_proj, gate_w, expert_w, rope, ramp, out):
    NB, N, _ = out.shape
    V, D = emb.shape
    HD = rope.shape[3]
    NH = D // HD
    NT = N // P
    C = D // P
    GROUPS = NH // 4
    SCALE = float(HD) ** -0.5
    KS = 3 * HD
    KM = KS + 2
    assert NT == 2 and C == 2 and NH == 16 and HD == 16 and NB % 2 == 0

    with ExitStack() as ctx:
        def sb(name, shape, dt=F32):
            return ctx.enter_context(nc.sbuf_tensor(name, shape, dt))

        def bank(name):
            return ctx.enter_context(nc.psum_tensor(name, [P, 512], F32))

        def sem(name):
            return ctx.enter_context(nc.semaphore(name))

        rope_sb = sb("rope_sb", [P, NT, 2, HD])
        ramp_sb = sb("ramp_sb", [P, N_EXP])
        ident = sb("ident", [P, P])
        ident_r = sb("ident_r", [P, P], F32R)
        neg_half = sb("neg_half", [P, NT])
        wqkv_h = sb("wqkv_h", [P, C, 3 * D], F32R)
        wqkv_l = sb("wqkv_l", [P, C, 3 * D], F32R)
        wp_h = sb("wp_h", [P, C, D], F32R)
        wp_l = sb("wp_l", [P, C, D], F32R)
        ew_raw = sb("ew_raw", [P, C, N_EXP * D])
        ew_h = sb("ew_h", [P, C, N_EXP * D], F32R)
        ew_l = sb("ew_l", [P, C, N_EXP * D], F32R)
        gw_raw = sb("gw_raw", [P, C, N_EXP])
        gw_parts = sb("gw_parts", [P, C, 2, N_EXP], F32R)
        ids = sb("ids", [P, NB * NT], I32)
        h0 = sb("h0", [P, NB * NT, D])
        f_st = sb("f_st", [P, NT, 6])
        f_mv = sb("f_mv", [P, NT, 2])
        f_ve = sb("f_ve", [P, NT])
        f_rs = sb("f_rs", [P, NT])
        xn = sb("xn", [P, NT, D])
        x_h = sb("x_h", [P, C, NT, P], F32R)
        x_l = sb("x_l", [P, C, NT, P], F32R)
        rope_a = sb("rope_a", [P, NT, 2 * NH, HD])
        rope_b = sb("rope_b", [P, NT, 2 * NH, HD])
        qk = sb("qk", [P, NT, 4, HD, 8])
        qk_h = sb("qk_h", [P, 4, N], F32R)
        qk_l = sb("qk_l", [P, 4, N], F32R)
        q_stack = [sb(f"q_stack{i}", [P, 8, N], F32R) for i in range(2)]
        k_stack = [sb(f"k_stack{i}", [P, 8, N], F32R) for i in range(2)]
        vals = [sb(f"vals{i}", [P, NT, NH, STRIP]) for i in range(2)]
        neg_max = sb("neg_max", [P, 2, NT, 8])
        max_parts = sb("max_parts", [P, 2, NT, 2, 8], F32R)
        ones = sb("ones", [16, N])
        max_rows = sb("max_rows", [16, 2, N], F32R)
        probs = sb("probs", [P, RING, NT, N])
        wqkv_raw = probs[:, 0:3, :, :].rearrange("p r t n -> p (r t n)").rearrange("p (c n) -> p c n", c=C)
        wp_raw = probs[:, 3, :, :]
        o_t = sb("o_t", [P, GROUPS, N])
        o_rs = sb("o_rs", [P, NT, NH])
        o_n = sb("o_n", [P, NT, NH, HD])
        o_h = sb("o_h", [P, C, NT, P], F32R)
        o_l = sb("o_l", [P, C, NT, P], F32R)
        h1 = sb("h1", [P, NT, D])
        g_st = sb("g_st", [P, NT, 6])
        g_mv = sb("g_mv", [P, NT, 2])
        g_ve = sb("g_ve", [P, NT])
        g_rs = sb("g_rs", [P, NT])
        yn = sb("yn", [P, NT, D])
        y_h = [sb(f"y_h{i}", [P, C, NT, P], F32R) for i in range(2)]
        y_l = [sb(f"y_l{i}", [P, C, NT, P], F32R) for i in range(2)]
        base = sb("base", [P, NT, D])
        gate_rows = sb("gate_rows", [2 * N_EXP, N])
        score = sb("score", [P, NT, N_EXP])
        top = sb("top", [P, NT, 8])
        top_at = sb("top_at", [P, NT, 8], U32)
        mask = sb("mask", [P, 2, NT, N_EXP])
        acc = sb("acc", [P, 2, NT, D])
        res = sb("res", [P, NT, D])

        s_bank = [bank("s_bank0"), bank("s_bank1")]
        f_bank = bank("f_bank")
        t_bank = [bank("t_bank0"), bank("t_bank1")]
        o_bank = bank("o_bank")
        m_bank = bank("m_bank")
        e_bank = bank("e_bank")

        ids_in, rope_in, wp_in, ew_in, gw_in = map(sem, "ids_in rope_in wp_in ew_in gw_in".split())
        wqkv_in = [sem(f"wqkv_in{c}") for c in range(C)]
        gathered = [sem(f"gathered{b}") for b in range(NB)]
        h_in = sem("h_in")
        h_zero, filled, pool_filled, ident_ok, identr_ok = map(sem, "h_zero filled pool_filled ident_ok identr_ok".split())
        wqkv_h_ok, wqkv_l_ok, wp_h_ok, wp_l_ok = map(sem, "wqkv_h_ok wqkv_l_ok wp_h_ok wp_l_ok".split())
        ew_h_ok, ew_l_ok, gw_h_ok, gw_l_ok = map(sem, "ew_h_ok ew_l_ok gw_h_ok gw_l_ok".split())
        f_stats, f_moments, f_var, f_rstd, f_normed = map(sem, "f_stats f_moments f_var f_rstd f_normed".split())
        xt_ps, xh_ok, xl_ok, v_ps, v_ok, qk_ps = map(sem, "xt_ps xh_ok xl_ok v_ps v_ok qk_ps".split())
        roped, rotated, qkt_ps, qkh_ok, qkl_ok, ones_ok = map(
            sem, "roped rotated qkt_ps qkh_ok qkl_ok ones_ok".split())
        ones_in = sem("ones_in")
        stack_in = [sem("stack_in0"), sem("stack_in1")]
        s_ps, max_ok, mh_ok, ml_ok, mt_ps, mt_ok = map(sem, "s_ps max_ok mh_ok ml_ok mt_ps mt_ok".split())
        m_in = [sem("m_in0"), sem("m_in1")]
        t_ps, exp_ok, o_ps, o_ok = map(sem, "t_ps exp_ok o_ps o_ok".split())
        ot_ps, ors_ok, on_ok, ont_ps, oh_ok, ol_ok, proj_ps, h1_ok = map(
            sem, "ot_ps ors_ok on_ok ont_ps oh_ok ol_ok proj_ps h1_ok".split())
        g_stats, g_moments, g_var, g_rstd, g_normed, base_ok = map(
            sem, "g_stats g_moments g_var g_rstd g_normed base_ok".split())
        yt_ps, yh_ok, yl_ok, gate_ps, gate_ok, gatet_ps, score_ok, top_ok, at_ok, mask_ok = map(
            sem, "yt_ps yh_ok yl_ok gate_ps gate_ok gatet_ps score_ok top_ok at_ok mask_ok".split())
        exp_ps, acc_ok, res_ok, out_ok = map(sem, "expert_ps acc_ok res_ok out_ok".split())

        def here(b, k):
            return not isinstance(b, int) or 0 <= b + k < NB

        def steps(engine, step):
            for b in range(-2, 2):
                step(b, b % 2)
            with engine.Fori(0, (NB - 4) // 2) as i:
                step(i * 2 + 2, 0)
                step(i * 2 + 3, 1)
            for b in range(NB - 2, NB + 2):
                step(b, b % 2)

        def early(b):
            return isinstance(b, int) and b < 4

        def front(b, what):
            if isinstance(b, int) and b == 1:
                at = dict(stats=-1, norm=-1, x=-1, x_low=-1, qk0=0, qk1=1, rotate0=1, rotate1=2,
                          t0=4, t1=5, low0=5, low1=6)
            elif early(b):
                at = dict(stats=0, norm=2, x=3, x_low=4, qk0=5, qk1=6, rotate0=6, rotate1=7,
                          t0=8, t1=9, low0=9, low1=10)
            else:
                at = dict(stats=0, norm=2, x=3, x_low=4, qk0=5, qk1=7, rotate0=6, rotate1=8,
                          t0=9, t1=11, low0=10, low1=12)
            return at[what]

        def front_bank(b, t):
            return e_bank if early(b) and t == 1 else f_bank

        def first(b):
            return isinstance(b, int) and b == -2

        def second(b):
            return isinstance(b, int) and b == -1

        def score_bank(b, h):
            banks = s_bank + t_bank if isinstance(b, int) and b == 0 else s_bank
            return banks[h % len(banks)]

        def maxima_slot(b):
            return 9 if isinstance(b, int) and b < 3 else 11

        def place(h):
            return 64 * (h // 8), h % 8

        def expert_banks(b):
            return [e_bank, f_bank] + s_bank if isinstance(b, int) and b >= NB - 3 else [e_bank]

        def unit_in(b, s):
            slots = (0, 2, 4, 6, 8, 10, 12, 14)
            if isinstance(b, int) and b == NB - 1:
                slots = (1, 3, 5, 7, 9, 11, 13, 14)
            if isinstance(b, int) and b == NB:
                slots = (0, 1, 2, 3, 5, 7, 8, 10)
            return slots.index(s) if s in slots else None

        def last(b):
            return isinstance(b, int) and b == NB - 1

        def post(b, what):
            if last(b):
                at = dict(o0=2, o1=2, norm0=3, norm1=3, on=4, o_low=5, proj=6, residual=7, stats=7, g_norm=8,
                          y=9, y_low=10, gate=11, gate_t=12, choose=12)
            else:
                at = dict(o0=2, o1=4, norm0=3, norm1=5, on=6, o_low=7, proj=8, residual=9, stats=10, g_norm=11,
                          y=12, y_low=13, gate=14, gate_t=15, choose=15)
            return at[what]

        def strips_bank(b, t):
            return t_bank[0] if last(b) and t == 1 else m_bank

        def wait(engine, semaphore, value):
            if not isinstance(value, int) or value > 0:
                engine.wait_ge(semaphore, value)

        def wait_apart(engine, semaphore, value):
            if not isinstance(value, int):
                value = engine.snap(engine.to_reg(value))
            engine.wait_ge(ident_ok, 1)
            wait(engine, semaphore, value)

        block = ctx.enter_context(nc.Block())

        @block.sync
        def _(sp):
            sp.sem_inc(out_ok, 16)
            sp.dma_start(ids[:, :], x).then_inc(ids_in, 16)
            for c in range(C):
                sp.dma_start(wqkv_raw[:, c, :], w_qkv[c * P:(c + 1) * P, :]).then_inc(wqkv_in[c], 16)
            sp.dma_start(rope_sb[:, :, :, :], rope).then_inc(rope_in, 16)
            sp.dma_start(ramp_sb[:, :], ramp).then_inc(rope_in, 16)
            sp.dma_start(gw_raw[:, :, :], gate_w).then_inc(gw_in, 16)
            for b in range(2):
                sp.wait_ge(gathered[b], 16 * NT)
            sp.dma_start(wp_raw, w_proj.rearrange("(c p) n -> p c n", p=P)).then_inc(wp_in, 16)
            sp.dma_start(ew_raw[:, :, :], expert_w).then_inc(ew_in, 16)

            def landed(b):
                sp.wait_ge(gathered[b], 16 * NT)
                sp.sem_inc(h_in, 1)

            def maximum(b, p, u):
                wait(sp, mt_ok, b * 2 + u + 1)
                r = 64 * u + KS
                sp.dma_start(q_stack[p][r:r + 2, :, :].bitcast(F32), max_rows[:, u, :].bitcast(F32)).then_inc(m_in[u], 16)

            def restack(b, p, half):
                taken = (b - 2) * NH + 8 * half + 8
                if not isinstance(b, int):
                    taken = sp.snap(sp.to_reg(taken))
                wait(sp, qkl_ok, b * NT + NT)
                wait(sp, t_ps, taken)
                for stack, group, blocks in ((q_stack[p], half, (qk_h, qk_l, qk_h)),
                                             (k_stack[p], 2 + half, (qk_h, qk_h, qk_l))):
                    for i, part in enumerate(blocks):
                        r = 64 * half + i * HD
                        sp.dma_start(stack[r:r + HD, :, :].bitcast(F32),
                                     part[:, group, :].bitcast(F32)).then_inc(stack_in[half], 16)

            def store(b):
                wait(sp, res_ok, b + 2)
                sp.dma_start(out[b].rearrange("(t p) d -> p t d", p=P), res[:, :, :]).then_inc(out_ok, 16)

            def step(b, p):
                if isinstance(b, int) and b == 1:
                    for k in range(4, NB):
                        landed(k)
                if here(b, 0):
                    maximum(b, p, 1)
                if here(b, 2) and early(b + 2):
                    restack(b + 2, p, 0)
                if here(b, 1):
                    maximum(b + 1, 1 - p, 0)
                if second(b):
                    restack(b + 2, p, 1)
                if here(b, 2) and not early(b + 2):
                    restack(b + 2, p, 0)
                if here(b, 2) and not second(b):
                    restack(b + 2, p, 1)
                if here(b, -2):
                    store(b - 2)

            sp.wait_ge(ones_ok, 1)
            for i in range(2):
                for half in range(2):
                    r = 64 * half + KS
                    sp.dma_start(k_stack[i][r:r + 2, :, :].bitcast(F32), ones[:, :]).then_inc(ones_in, 16)
            steps(sp, step)
            sp.wait_ge(out_ok, 16 * (NB + 1))

        @block.gpsimd
        def _(pool):
            g = nc.gpsimd
            pool.sem_inc(res_ok, 1)
            g.memset(ident[:, :], 0.0).then_inc(pool_filled, 1)
            g.memset(neg_half[:, :], -0.5).then_inc(pool_filled, 1)
            pool.wait_ge(pool_filled, 2)
            g.affine_select(out=ident[:, :], in_=ident[:, :], compare_op=ALU.not_equal, fill=1.0, base=0,
                            pattern=[[-1, P]], channel_multiplier=1).then_inc(ident_ok, 1)
            pool.wait_ge(ids_in, 16)

            def gather(b):
                for j in range(b * NT, (b + 1) * NT):
                    pool.wait_ge(h_zero, b + 1)
                    g.indirect_dma_start(h0[:, j, :], None, emb, bass.IndirectOffsetOnAxis(ap=ids[:, j:j + 1], axis=0),
                                         bounds_check=V - 1, oob_is_err=False).then_inc(gathered[b], 16)

            def f_rs_of(b):
                wait_apart(pool, f_moments, b * NT + NT)
                g.tensor_scalar(f_ve[:, :], f_mv[:, :, 1], EPS, None, ALU.add).then_inc(f_var, 1)
                wait(pool, f_var, b + 1)
                g.tensor_tensor(f_rs[:, :], f_ve[:, :], neg_half[:, :], ALU.pow).then_inc(f_rstd, 1)

            def rotated_sum(b, t):
                wait(pool, roped, b * 2 * NT + 2 * t + 2)
                g.tensor_tensor(qk[:, t, :, :, :].rearrange("p g d j -> p g j d"),
                                rope_a[:, t, :, :].rearrange("p (g j) d -> p g j d", j=8),
                                rope_b[:, t, :, :].rearrange("p (g j) d -> p g j d", j=8),
                                ALU.add).then_inc(rotated, 1)

            def g_rs_of(b):
                wait_apart(pool, g_moments, b * NT + NT)
                g.tensor_scalar(g_ve[:, :], g_mv[:, :, 1], EPS, None, ALU.add).then_inc(g_var, 1)
                wait(pool, g_var, b + 1)
                g.tensor_tensor(g_rs[:, :], g_ve[:, :], neg_half[:, :], ALU.pow).then_inc(g_rstd, 1)

            def residuals(b):
                wait(pool, g_normed, b * NT + NT)
                g.tensor_tensor(base[:, :, :], h1[:, :, :], yn[:, :, :], ALU.add).then_inc(base_ok, 1)

            def finish(b):
                wait(pool, acc_ok, b * 16 + 17)
                wait(pool, out_ok, b * 16 + 16)
                g.tensor_tensor(res[:, :, :], acc[:, 0, :, :], acc[:, 1, :, :], ALU.add).then_inc(res_ok, 1)

            def expert_weights(ks):
                for k in ks:
                    pool.wait_ge(ew_h_ok, k + 1)
                    w = slice(k % 4 * 2 * D, (k % 4 + 1) * 2 * D)
                    g.tensor_tensor(ew_l[:, k // 4, w], ew_raw[:, k // 4, w], ew_h[:, k // 4, w].bitcast(F32),
                                    ALU.subtract).then_inc(ew_l_ok, 1)

            def gate_weights():
                pool.wait_ge(gw_h_ok, 1)
                g.tensor_tensor(gw_parts[:, :, 1, :], gw_raw[:, :, :], gw_parts[:, :, 0, :].bitcast(F32),
                                ALU.subtract).then_inc(gw_l_ok, 1)

            def step(b, p):
                if here(b, 2):
                    f_rs_of(b + 2)
                if isinstance(b, int) and b == -2:
                    gather(2)
                if here(b, 2):
                    rotated_sum(b + 2, 0)
                    rotated_sum(b + 2, 1)
                if isinstance(b, int) and b == -2:
                    gather(3)
                if isinstance(b, int) and b in (-1, 0):
                    gather(2 * b + 6)
                    gather(2 * b + 7)
                if here(b, -1):
                    g_rs_of(b - 1)
                    residuals(b - 1)
                if here(b, -2):
                    finish(b - 2)
                if isinstance(b, int) and b == -1:
                    gate_weights()
                if isinstance(b, int) and b in (-1, 0):
                    expert_weights(range(4 * b + 4, 4 * b + 8))

            gather(0)
            gather(1)
            steps(pool, step)

        @block.tensor
        def _(pe):
            mm = nc.tensor.matmul
            tr = nc.tensor.transpose

            def product(o, xh, xl, wh, wl):
                n = 0
                for c in range(C):
                    for a, w in ((xh, wh), (xl, wh), (xh, wl)):
                        m = mm(o, a(c), w(c), start=(n == 0), stop=(n == 3 * C - 1))
                        n += 1
                return m

            def x_transpose(b):
                wait(pe, v_ok, b)
                wait(pe, f_normed, b * NT + NT)
                for c in range(C):
                    for t in range(NT):
                        k = (c * NT + t) * P
                        m = tr(f_bank[:, k:k + P], xn[:, t, c * P:(c + 1) * P], ident[:, :])
                m.then_inc(xt_ps, 1)

            def project_v(b):
                if isinstance(b, int) and b == 0:
                    wait(pe, qkl_ok, NT)
                for t in range(NT):
                    m = product(f_bank[:, t * D:(t + 1) * D], lambda c: x_h[:, c, t, :], lambda c: x_l[:, c, t, :],
                                lambda c: wqkv_h[:, c, 2 * D:3 * D], lambda c: wqkv_l[:, c, 2 * D:3 * D])
                m.then_inc(v_ps, 1)

            def project_qk(b, t):
                if t == 0:
                    if isinstance(b, int) and b == 0:
                        pe.wait_ge(wqkv_l_ok, C)
                    wait(pe, xl_ok, b + 1)
                elif early(b):
                    wait(pe, qkl_ok, b * NT)
                else:
                    wait(pe, roped, b * 2 * NT + 2)
                product(front_bank(b, t)[:, :], lambda c: x_h[:, c, t, :], lambda c: x_l[:, c, t, :],
                        lambda c: wqkv_h[:, c, 0:2 * D], lambda c: wqkv_l[:, c, 0:2 * D]).then_inc(qk_ps, 1)

            def qk_transpose(b, t):
                if early(b):
                    wait(pe, roped, b * 2 * NT + 2 * t + 2)
                elif t == 0:
                    wait(pe, roped, b * 2 * NT + 2 * NT)
                else:
                    wait(pe, qkh_ok, b * NT + 1)
                    wait(pe, qkl_ok, b * NT + 1)
                wait(pe, rotated, b * NT + t + 1)
                for i in range(4):
                    m = tr(front_bank(b, t)[:, i * P:(i + 1) * P], qk[:, t, i, :, :].rearrange("p d j -> p (d j)"),
                           ident[:, :])
                m.then_inc(qkt_ps, 1)

            def scores(b, p, h):
                if h % 8 == 0:
                    wait(pe, stack_in[h // 8], b * 96 + 96)
                if not (isinstance(b, int) and b == 0 and h < 4):
                    wait(pe, max_ok, b * NH + h - (3 if isinstance(b, int) and b == 0 else 1))
                r, pair = place(h)
                for t in range(NT):
                    m = mm(score_bank(b, h)[:, t * N:(t + 1) * N], q_stack[p][r:r + KS, pair, t * P:(t + 1) * P],
                           k_stack[p][r:r + KS, pair, :], start=True, stop=True)
                m.then_inc(s_ps, 1)

            def max_transpose(b, u):
                wait(pe, o_ok, (b - 1) * GROUPS + (4 if u else 1 if maxima_slot(b) == 9 else 2))
                wait(pe, ml_ok, b * 2 + u + 1)
                for t in range(NT):
                    m = tr(o_bank[0:16, N + t * P:N + (t + 1) * P].bitcast(F32R),
                           max_parts[:, u, t, :, :].rearrange("p a b -> p (a b)"), ident_r[:, :])
                m.then_inc(mt_ps, 1)

            def t_scores(b, p, h):
                if h == 0 and isinstance(b, int) and b == 0:
                    pe.wait_ge(ones_in, 64)
                    pe.wait_ge(wp_l_ok, 1)
                    pe.wait_ge(gw_l_ok, 1)
                if h % 8 == 0:
                    wait(pe, m_in[h // 8], b * 16 + 16)
                wait(pe, exp_ok, b * NH + h - 1)
                if isinstance(b, int) and b == 0 and h < 2:
                    pe.wait_ge(max_ok, NH - 1 + h)
                r, pair = place(h)
                for c in range(NT):
                    m = mm(t_bank[h % 2][:, c * N:(c + 1) * N], k_stack[p][r:r + KM, pair, c * P:(c + 1) * P],
                           q_stack[p][r:r + KM, pair, :], start=True, stop=True)
                m.then_inc(t_ps, 1)

            def outs_free(b, g):
                if g == 0:
                    wait(pe, mt_ok, b * 2 + 2)
                elif here(b, 1):
                    wait(pe, mt_ok, b * 2 + 3)
                else:
                    wait(pe, o_ok, b * GROUPS + g)

            def outputs(b, p, g):
                wait(pe, exp_ok, b * NH + 4 * g + 4)
                if g == 0 or g == 1 and maxima_slot(b + 1) == 9 or g == 2 and maxima_slot(b + 1) == 11:
                    outs_free(b, g)
                else:
                    wait(pe, o_ok, b * GROUPS + g)
                for c in range(NT):
                    for j in range(4):
                        m = mm(o_bank[STRIP * j:STRIP * (j + 1), 0:N], vals[p][:, c, 4 * g + j, :],
                               probs[:, (4 * g + j) % RING, c, :], start=(c == 0), stop=(c == NT - 1),
                               skip_group_check=True)
                m.then_inc(o_ps, 1)

            def o_transpose(b, t):
                if t == 0:
                    wait(pe, o_ok, b * GROUPS + GROUPS)
                    wait(pe, score_ok, b)
                elif not last(b):
                    wait(pe, on_ok, b * NT + 1)
                for g in range(GROUPS):
                    m = tr(strips_bank(b, t)[:, g * P:(g + 1) * P], o_t[:, g, t * P:(t + 1) * P], ident[:, :])
                m.then_inc(ot_ps, 1)

            def on_transpose(b):
                wait(pe, on_ok, b * NT + NT)
                for c in range(C):
                    for t in range(NT):
                        k = (c * NT + t) * P
                        m = tr(m_bank[:, k:k + P],
                               o_n[:, t, c * NH // C:(c + 1) * NH // C, :].rearrange("p h d -> p (h d)"), ident[:, :])
                m.then_inc(ont_ps, 1)

            def out_project(b):
                wait(pe, ol_ok, b + 1)
                for t in range(NT):
                    m = product(m_bank[:, t * D:(t + 1) * D], lambda c: o_h[:, c, t, :], lambda c: o_l[:, c, t, :],
                                lambda c: wp_h[:, c, :], lambda c: wp_l[:, c, :])
                m.then_inc(proj_ps, 1)

            def y_transpose(b):
                wait(pe, g_normed, b * NT + NT)
                for c in range(C):
                    for t in range(NT):
                        k = (c * NT + t) * P
                        m = tr(m_bank[:, k:k + P], yn[:, t, c * P:(c + 1) * P], ident[:, :])
                m.then_inc(yt_ps, 1)

            def gate(b, p):
                wait(pe, yl_ok, b + 1)
                for c in range(C):
                    for part in (y_h[p], y_l[p]):
                        m = mm(m_bank[0:2 * N_EXP, 0:N], gw_parts[:, c, :, :].rearrange("p a e -> p (a e)"),
                               part[:, c, :, :].rearrange("p t n -> p (t n)"),
                               start=(c == 0 and part is y_h[p]), stop=(c == C - 1 and part is y_l[p]))
                m.then_inc(gate_ps, 1)

            def gate_transpose(b):
                wait_apart(pe, gate_ok, b + 1)
                for t in range(NT):
                    m = tr(m_bank[:, N + t * 2 * N_EXP:N + (t + 1) * 2 * N_EXP], gate_rows[:, t * P:(t + 1) * P],
                           ident[0:2 * N_EXP, 0:2 * N_EXP])
                m.then_inc(gatet_ps, 1)

            def experts(b, p, n, banks):
                u, t = n // NT, n % NT
                if n == 0 and isinstance(b, int) and b == 0:
                    pe.wait_ge(ew_l_ok, 8)
                if isinstance(b, int) and b == NB - 3 and n == 1:
                    wait(pe, max_ok, NB * NH)
                same = isinstance(b, int) and b > NB - 3
                wait(pe, acc_ok, b * 16 + 2 * (n - len(banks) + 1 if same else max(n - len(banks) + 1, 0)) + 1)
                product(banks[n % len(banks)][:, :], lambda c: y_h[p][:, c, t, :], lambda c: y_l[p][:, c, t, :],
                        lambda c: ew_h[:, c, 2 * u * D:2 * (u + 1) * D],
                        lambda c: ew_l[:, c, 2 * u * D:2 * (u + 1) * D]).then_inc(exp_ps, 1)

            def norm_and_project(b, s):
                if here(b, 2):
                    if s == front(b + 2, "x"):
                        x_transpose(b + 2)
                    for t in range(NT):
                        if s == front(b + 2, f"qk{t}"):
                            project_qk(b + 2, t)
                    for t in range(NT):
                        if s == front(b + 2, f"t{t}"):
                            qk_transpose(b + 2, t)

            def step(b, p):
                norm_and_project(b, -1)
                for s in range(NH):
                    if here(b, 0):
                        t_scores(b, p, s)
                    if here(b, 1):
                        scores(b + 1, 1 - p, s)
                    if here(b, 0) and s == 3:
                        max_transpose(b, 1)
                    if first(b) and s == 15:
                        project_v(0)
                    if here(b, 1) and s == maxima_slot(b + 1):
                        max_transpose(b + 1, 0)
                    if here(b, -1):
                        if s == post(b - 1, "o1") and not last(b - 1):
                            o_transpose(b - 1, 1)
                        if s == post(b - 1, "on"):
                            on_transpose(b - 1)
                        if s == post(b - 1, "proj") and last(b - 1):
                            out_project(b - 1)
                        if s == post(b - 1, "y"):
                            y_transpose(b - 1)
                        if s == post(b - 1, "gate"):
                            gate(b - 1, 1 - p)
                        if s == post(b - 1, "gate_t"):
                            gate_transpose(b - 1)
                    norm_and_project(b, s)
                    if here(b, -1) and s == 1:
                        outputs(b - 1, 1 - p, 3)
                    if here(b, 1) and s == 1 and not second(b):
                        project_v(b + 1)
                    if here(b, 0) and s in (5, 9, 13):
                        outputs(b, p, (s - 5) // 4)
                    if here(b, -2) and unit_in(b, s) is not None:
                        experts(b - 2, p, unit_in(b, s), expert_banks(b - 2))
                    if here(b, -1) and s == post(b - 1, "o0"):
                        o_transpose(b - 1, 0)
                        if last(b - 1):
                            o_transpose(b - 1, 1)
                    if here(b, -1) and s == post(b - 1, "proj") and not last(b - 1):
                        out_project(b - 1)

            pe.wait_ge(ident_ok, 1)
            pe.wait_ge(identr_ok, 1)
            pe.wait_ge(filled, 2)
            steps(pe, step)

        @block.scalar
        def _(act):
            def copy(o, i):
                return nc.scalar.activation(o, i, ACT.Copy)

            def x_high(b):
                wait(act, xt_ps, b + 1)
                copy(x_h[:, :, :, :].rearrange("p c t n -> p (c t n)"), f_bank[:, :]).then_inc(xh_ok, 1)

            def values(b, p):
                wait(act, v_ps, b + 1)
                copy(vals[p][:, :, :, 0:HD], f_bank[:, :].rearrange("p (t h d) -> p t h d", t=NT, h=NH)).then_inc(v_ok, 1)

            def qk_high(b, t):
                wait(act, qkt_ps, b * NT + t + 1)
                for half in range(2):
                    wait(act, stack_in[half], b * 96)
                copy(qk_h[:, :, t * P:(t + 1) * P],
                     front_bank(b, t)[:, :].rearrange("p (g n) -> p g n", g=4)).then_inc(qkh_ok, 1)

            def max_row(b, u):
                wait(act, mt_ps, b * 2 + u + 1)
                copy(max_rows[:, u, :], o_bank[0:16, N:2 * N]).then_inc(mt_ok, 1)

            def exp(b, h):
                wait(act, t_ps, b * NH + h + 1)
                if h % 4 == 0:
                    wait(act, o_ps, b * GROUPS + h // 4 - 1)
                nc.scalar.activation(probs[:, h % RING, :, :].rearrange("p c n -> p (c n)"), t_bank[h % 2][:, :],
                                     ACT.Exp, scale=SCALE).then_inc(exp_ok, 1)

            def outputs(b, g):
                wait(act, o_ps, b * GROUPS + g + 1)
                if g == 0:
                    wait(act, ot_ps, b * NT)
                copy(o_t[:, g, :], o_bank[:, 0:N]).then_inc(o_ok, 1)

            def o_high(b):
                wait(act, ont_ps, b + 1)
                copy(o_h[:, :, :, :].rearrange("p c t n -> p (c t n)"), m_bank[:, :]).then_inc(oh_ok, 1)

            def y_high(b, p):
                wait(act, yt_ps, b + 1)
                copy(y_h[p][:, :, :, :].rearrange("p c t n -> p (c t n)"), m_bank[:, :]).then_inc(yh_ok, 1)

            def gate_row(b):
                wait(act, gate_ps, b + 1)
                copy(gate_rows[:, :], m_bank[0:2 * N_EXP, 0:N]).then_inc(gate_ok, 1)

            def expert_weights(k):
                if k == 0:
                    act.wait_ge(ew_in, 16)
                w = slice(k % 4 * 2 * D, (k % 4 + 1) * 2 * D)
                copy(ew_h[:, k // 4, w], ew_raw[:, k // 4, w]).then_inc(ew_h_ok, 1)

            def step(b, p):
                if second(b):
                    x_high(b + 2)
                for s in range(NH):
                    if here(b, 0):
                        exp(b, s)
                    if here(b, 0) and s == 3:
                        max_row(b, 1)
                    if first(b) and s == 15:
                        values(0, 0)
                    if here(b, -1) and s == 1:
                        outputs(b - 1, 3)
                    if here(b, 1) and s == 1 and not second(b):
                        values(b + 1, 1 - p)
                    if here(b, 2) and s == front(b + 2, "x"):
                        x_high(b + 2)
                    if here(b, 0) and s in (6, 10, 14):
                        outputs(b, (s - 6) // 4)
                    if here(b, -1) and s == post(b - 1, "on"):
                        o_high(b - 1)
                    for t in range(NT):
                        if here(b, 2) and s == front(b + 2, f"t{t}"):
                            qk_high(b + 2, t)
                    if here(b, 1) and s == maxima_slot(b + 1):
                        max_row(b + 1, 0)
                    if here(b, -1) and s == post(b - 1, "y"):
                        y_high(b - 1, 1 - p)
                    if here(b, -1) and s == post(b - 1, "gate"):
                        gate_row(b - 1)
                    if second(b) and s % 2:
                        expert_weights(s // 2)
                    if isinstance(b, int) and b == -2 and s == 4:
                        act.wait_ge(wp_in, 16)
                        copy(wp_h[:, :, :], wp_raw).then_inc(wp_h_ok, 1)
                        act.wait_ge(gw_in, 16)
                        copy(gw_parts[:, :, 0, :], gw_raw[:, :, :]).then_inc(gw_h_ok, 1)

            for c in range(C):
                act.wait_ge(wqkv_in[c], 16)
                copy(wqkv_h[:, c, :], wqkv_raw[:, c, :]).then_inc(wqkv_h_ok, 1)
            act.wait_ge(filled, 2)
            steps(act, step)

        @block.vector
        def _(dve):
            v = nc.vector

            def norm_stats(b, src, st, mv, stats, moments):
                for t in range(NT):
                    v.bn_stats(st[:, t, :], src(t)).then_inc(stats, 1)
                for t in range(NT):
                    wait_apart(dve, stats, b * NT + t + 1)
                    v.bn_aggr(mv[:, t, :], st[:, t, :]).then_inc(moments, 1)

            def f_norm_a(b):
                if early(b):
                    dve.wait_ge(gathered[b], 16 * NT)
                else:
                    wait(dve, h_in, b - 3)
                norm_stats(b, lambda t: h0[:, b * NT + t, :], f_st, f_mv, f_stats, f_moments)

            def f_norm_b(b):
                wait(dve, f_rstd, b + 1)
                for t in range(NT):
                    v.tensor_scalar(xn[:, t, :], h0[:, b * NT + t, :], f_mv[:, t, 0:1], f_rs[:, t:t + 1],
                                    ALU.subtract, ALU.mult).then_inc(f_normed, 1)

            def x_low(b):
                wait(dve, xh_ok, b + 1)
                v.tensor_tensor(x_l[:, :, :, :].rearrange("p c t n -> p (c t n)"), f_bank[:, :],
                                x_h[:, :, :, :].rearrange("p c t n -> p (c t n)").bitcast(F32),
                                ALU.subtract).then_inc(xl_ok, 1)

            def rotate(b, t):
                if t == 0 and isinstance(b, int) and b == 0:
                    dve.wait_ge(rope_in, 32)
                wait(dve, qk_ps, b * NT + t + 1)
                src = front_bank(b, t)[:, :].rearrange("p (h d) -> p h d", d=HD)
                cos = rope_sb[:, t, 0:1, :].broadcast_to([P, 2 * NH, HD])
                v.tensor_tensor(rope_a[:, t, :, :], src, cos, ALU.mult).then_inc(roped, 1)
                swap = front_bank(b, t)[:, :].rearrange("p (h i two) -> p h i two", two=2, i=HD // 2)[:, :, :, ::-1]
                sin = rope_sb[:, t, 1:2, :].broadcast_to([P, 2 * NH, HD]).rearrange("p h (i two) -> p h i two", two=2)
                v.tensor_tensor(rope_b[:, t, :, :].rearrange("p h (i two) -> p h i two", two=2), swap, sin,
                                ALU.mult).then_inc(roped, 1)

            def qk_low(b, t):
                wait(dve, qkh_ok, b * NT + t + 1)
                v.tensor_tensor(qk_l[:, :, t * P:(t + 1) * P], front_bank(b, t)[:, :].rearrange("p (g n) -> p g n", g=4),
                                qk_h[:, :, t * P:(t + 1) * P].bitcast(F32), ALU.subtract).then_inc(qkl_ok, 1)

            def maximum(b, h):
                wait(dve, s_ps, b * NH + h + 1)
                v.tensor_reduce(neg_max[:, h // 8, :, h % 8],
                                score_bank(b, h)[:, :].rearrange("p (t n) -> p t n", t=NT), AX.X, ALU.max,
                                negate=True).then_inc(max_ok, 1)

            def max_split(b, u):
                wait(dve, max_ok, b * NH + 8 * u + 8)
                v.tensor_copy(max_parts[:, u, :, 0, :], neg_max[:, u, :, :]).then_inc(mh_ok, 1)
                wait(dve, mh_ok, b * 2 + u + 1)
                v.tensor_tensor(max_parts[:, u, :, 1, :], neg_max[:, u, :, :],
                                max_parts[:, u, :, 0, :].bitcast(F32), ALU.subtract).then_inc(ml_ok, 1)

            def o_norm(b, t):
                wait(dve, ot_ps, b * NT + t + 1)
                o = strips_bank(b, t)[:, :].rearrange("p (h s) -> p h s", s=STRIP)
                v.reciprocal(o_rs[:, t, :], o[:, :, HD]).then_inc(ors_ok, 1)
                wait(dve, ors_ok, b * NT + t + 1)
                v.tensor_tensor(o_n[:, t, :, :], o[:, :, 0:HD],
                                o_rs[:, t, :].rearrange("p (h o) -> p h o", o=1).broadcast_to([P, NH, HD]),
                                ALU.mult).then_inc(on_ok, 1)

            def o_low(b):
                wait(dve, oh_ok, b + 1)
                v.tensor_tensor(o_l[:, :, :, :].rearrange("p c t n -> p (c t n)"), m_bank[:, :],
                                o_h[:, :, :, :].rearrange("p c t n -> p (c t n)").bitcast(F32),
                                ALU.subtract).then_inc(ol_ok, 1)

            def residual(b):
                wait(dve, proj_ps, b + 1)
                for t in range(NT):
                    v.tensor_tensor(h1[:, t, :], m_bank[:, t * D:(t + 1) * D], h0[:, b * NT + t, :],
                                    ALU.add).then_inc(h1_ok, 1)

            def g_norm_a(b):
                wait(dve, h1_ok, b * NT + NT)
                norm_stats(b, lambda t: h1[:, t, :], g_st, g_mv, g_stats, g_moments)

            def g_norm_b(b):
                wait(dve, g_rstd, b + 1)
                for t in range(NT):
                    v.tensor_scalar(yn[:, t, :], h1[:, t, :], g_mv[:, t, 0:1], g_rs[:, t:t + 1],
                                    ALU.subtract, ALU.mult).then_inc(g_normed, 1)

            def y_low(b, p):
                wait(dve, yh_ok, b + 1)
                v.tensor_tensor(y_l[p][:, :, :, :].rearrange("p c t n -> p (c t n)"), m_bank[:, :],
                                y_h[p][:, :, :, :].rearrange("p c t n -> p (c t n)").bitcast(F32),
                                ALU.subtract).then_inc(yl_ok, 1)

            def choose(b, p):
                wait(dve, gatet_ps, b + 1)
                both = m_bank[:, N:N + NT * 2 * N_EXP].rearrange("p (t a e) -> p t e a", t=NT, a=2)
                v.tensor_reduce(score[:, :, :], both, AX.X, ALU.add).then_inc(score_ok, 1)
                wait_apart(dve, score_ok, b + 1)
                for t in range(NT):
                    v.max(top[:, t, :], score[:, t, :]).then_inc(top_ok, 1)
                for t in range(NT):
                    wait_apart(dve, top_ok, b * NT + t + 1)
                    v.max_index(top_at[:, t, :], top[:, t, :], score[:, t, :]).then_inc(at_ok, 1)
                for t in range(NT):
                    wait(dve, at_ok, b * NT + t + 1)
                    v.tensor_scalar(mask[:, p, t, :], ramp_sb[:, :], top_at[:, t, 0:1], None,
                                    ALU.is_equal).then_inc(mask_ok, 1)

            def select(b, p, n, banks):
                u, t = n // NT, n % NT
                wait(dve, exp_ps, b * 8 + n + 1)
                if n == 0:
                    wait(dve, mask_ok, b * NT + NT)
                    wait(dve, base_ok, b + 1)
                    wait(dve, res_ok, b + 1)
                for j in range(2):
                    e = 2 * u + j
                    y = banks[n % len(banks)][:, j * D:(j + 1) * D]
                    if u == 0 and j == 1:
                        v.tensor_scalar(acc[:, 1, t, :], y, mask[:, p, t, e:e + 1], None, ALU.mult).then_inc(acc_ok, 1)
                        continue
                    if u > 0:
                        wait(dve, acc_ok, b * 16 + 2 * (n - 2) + j + 2)
                    v.scalar_tensor_tensor(out=acc[:, j, t, :], in0=y, scalar=mask[:, p, t, e:e + 1],
                                           in1=base[:, t, :] if u == 0 else acc[:, j, t, :],
                                           op0=ALU.mult, op1=ALU.add).then_inc(acc_ok, 1)

            def weights_low(w_l, raw, w_h, done):
                v.tensor_tensor(w_l, raw, w_h.bitcast(F32), ALU.subtract).then_inc(done, 1)

            def norm_and_rotate(b, s):
                if not here(b, 2):
                    return
                if s == front(b + 2, "stats"):
                    f_norm_a(b + 2)
                if first(b) and s == 0:
                    for c in range(C):
                        dve.wait_ge(wqkv_h_ok, c + 1)
                        weights_low(wqkv_l[:, c, :], wqkv_raw[:, c, :], wqkv_h[:, c, :], wqkv_l_ok)
                if s == front(b + 2, "norm"):
                    f_norm_b(b + 2)
                if s == front(b + 2, "x_low"):
                    x_low(b + 2)
                if first(b) and s == 5:
                    dve.wait_ge(wp_h_ok, 1)
                    weights_low(wp_l[:, :, :], wp_raw, wp_h[:, :, :], wp_l_ok)
                for t in range(NT):
                    if s == front(b + 2, f"rotate{t}"):
                        rotate(b + 2, t)
                for t in range(NT):
                    if s == front(b + 2, f"low{t}"):
                        qk_low(b + 2, t)

            def step(b, p):
                norm_and_rotate(b, -1)
                for s in range(NH):
                    if s > 0 and here(b, 1):
                        maximum(b + 1, s - 1)
                        if s == 8:
                            max_split(b + 1, 0)
                    if s == 0 and here(b, 0):
                        maximum(b, NH - 1)
                        max_split(b, 1)
                    if here(b, -1) and s == post(b - 1, "stats") and not last(b - 1):
                        g_norm_a(b - 1)
                    if here(b, -1) and s == post(b - 1, "g_norm"):
                        g_norm_b(b - 1)
                    if here(b, -2) and s > 0 and unit_in(b, s - 1) is not None:
                        select(b - 2, p, unit_in(b, s - 1), expert_banks(b - 2))
                    norm_and_rotate(b, s)
                    if here(b, -1):
                        for t in range(NT):
                            if s == post(b - 1, f"norm{t}"):
                                o_norm(b - 1, t)
                        if s == post(b - 1, "o_low"):
                            o_low(b - 1)
                        if s == post(b - 1, "residual"):
                            residual(b - 1)
                            if last(b - 1):
                                g_norm_a(b - 1)
                        if s == post(b - 1, "y_low"):
                            y_low(b - 1, 1 - p)
                        if s == post(b - 1, "choose"):
                            choose(b - 1, 1 - p)

            dve.sem_inc(acc_ok, 1)
            for b in range(NB):
                v.memset(h0[:, b * NT:(b + 1) * NT, :], 0.0).then_inc(h_zero, 1)
            v.memset(ones[:, :], 1.0).then_inc(ones_ok, 1)
            dve.wait_ge(ident_ok, 1)
            v.tensor_copy(ident_r[:, :], ident[:, :]).then_inc(identr_ok, 1)
            for i in range(2):
                v.memset(vals[i][:, :, :, HD:STRIP], 0.0).then_inc(h_zero, 1)
            dve.wait_ge(h_zero, NB + 2)
            for i in range(2):
                v.memset(vals[i][:, :, :, HD:HD + 1], 1.0).then_inc(filled, 1)
            steps(dve, step)


def kernel(x, L0_tok_embeddings, L0_attn_w_qkv, L0_attn_w_proj, L0_ffn_gate_w, L0_ffn_expert_w):
    import concourse.bacc as bacc
    from concourse.bass_utils import run_bass_kernel_spmd

    def rows(a):
        a = a.reshape(-1, P, *a.shape[1:])
        return np.ascontiguousarray(a.swapaxes(0, 1))

    d = L0_tok_embeddings.shape[1]
    arrays = {
        "x": rows(np.asarray(x).reshape(-1)),
        "emb": np.ascontiguousarray(L0_tok_embeddings),
        "w_qkv": np.ascontiguousarray(L0_attn_w_qkv),
        "w_proj": np.ascontiguousarray(L0_attn_w_proj),
        "gate_w": rows(np.asarray(L0_ffn_gate_w).T),
        "expert_w": rows(np.asarray(L0_ffn_expert_w).transpose(2, 0, 1).reshape(d, -1)),
        "rope": rope_tables(x.shape[1], 16),
        "ramp": np.ascontiguousarray(np.broadcast_to(np.arange(N_EXP, dtype=np.float32), (P, N_EXP))),
    }
    nc = bacc.Bacc("TRN2", target_bir_lowering=False, num_devices=1)
    args = [nc.dram_tensor(f"in_{n}", a.shape, mybir.dt.from_np(a.dtype), kind="ExternalInput").ap()
            for n, a in arrays.items()]
    out = nc.dram_tensor("out", (*x.shape, d), F32, kind="ExternalOutput").ap()
    tower(nc, *args, out)
    r = run_bass_kernel_spmd(nc, [{f"in_{n}": a for n, a in arrays.items()}], core_ids=[0])
    return r.results[0]["out"]
```
